# Optimizing a Trainium2 kernel written in Bass

```python
import numpy as np
import jax
import jax.numpy as jnp

def _softmax(x, axis=-1):
    return jax.nn.softmax(x, axis=axis)

def _gelu(x):
    return jax.nn.gelu(x, approximate=True)

def _silu(x):
    return jax.nn.silu(x)

def _sigmoid(x):
    return jax.nn.sigmoid(x)

def _layernorm(x, axis=-1, eps=1e-05):
    m = jnp.mean(x, axis=axis, keepdims=True)
    v = jnp.var(x, axis=axis, keepdims=True)
    return (x - m) / jnp.sqrt(v + eps)

def _scatter_add(tgt, idx, src, axis=0):
    return tgt.at[idx].add(src)

def _segment_sum(src, seg, n):
    return jax.ops.segment_sum(src, seg, n)
kernel_name = 'mk_conv_preact_d2_conv_nhwc64_r2_232b6f'

def setup_inputs(seed: int=0):
    np.random.seed(seed)
    _w = jnp.asarray

    def _rec_inputs():
        import jax
        import jax.numpy as jnp
        _gk = jax.random.key(seed)
        x = -0.000125 + 0.9999 * jax.random.normal(jax.random.fold_in(_gk, 1), (8, 128, 128, 32), jnp.float32)
        return x
    x = _rec_inputs()

    def _L0_conv_setup():
        import jax, jax.numpy as jnp
        import numpy as np
        LEAK = 0.3
        BN_EPS = 0.001

        def _conv(x, w, b, dil=1):
            y = jax.lax.conv_general_dilated(x, w, window_strides=(1, 1), padding='SAME', rhs_dilation=(dil, dil), dimension_numbers=('NHWC', 'HWIO', 'NHWC'))
            return y + b

        def _lrelu(x):
            return jnp.where(x >= 0, x, LEAK * x)

        def _dwt_haar(x):
            a = x[:, ::2, ::2, :]
            b = x[:, ::2, 1::2, :]
            c = x[:, 1::2, ::2, :]
            d = x[:, 1::2, 1::2, :]
            LL = (a + b + c + d) * 0.5
            LH = (c + d - a - b) * 0.5
            HL = (b + d - a - c) * 0.5
            HH = (a - b - c + d) * 0.5
            return (LL, LH, HL, HH)

        def _idwt_haar(LL, LH, HL, HH):
            a = (LL - LH - HL + HH) * 0.5
            b = (LL - LH + HL - HH) * 0.5
            c = (LL + LH - HL - HH) * 0.5
            d = (LL + LH + HL + HH) * 0.5
            B, h, w, C = LL.shape
            top = jnp.stack([a, b], axis=3).reshape(B, h, 2 * w, C)
            bot = jnp.stack([c, d], axis=3).reshape(B, h, 2 * w, C)
            return jnp.stack([top, bot], axis=2).reshape(B, 2 * h, 2 * w, C)
        key = jax.random.key(seed)
        ks = jax.random.split(key, 32)
        B, H, W, C, F = (8, 128, 128, 32, 32)
        s = 0.05

        def nrm(k, shape, scale=s):
            return jax.random.normal(k, shape, jnp.float32) * scale
        inp = {'x': jax.random.normal(ks[0], (B, H, W, C), jnp.float32), 'w15': nrm(ks[1], (5, 5, 3 * C, F)), 'b15': nrm(ks[2], (F,)), 'w25': nrm(ks[3], (5, 5, F, F)), 'b25': nrm(ks[4], (F,)), 'w13': nrm(ks[5], (3, 3, 3 * C, F)), 'b13': nrm(ks[6], (F,)), 'w23': nrm(ks[7], (3, 3, F, F)), 'b23': nrm(ks[8], (F,)), 'w12': nrm(ks[9], (2, 2, 3 * C, F)), 'b12': nrm(ks[10], (F,)), 'w22': nrm(ks[11], (2, 2, F, F)), 'b22': nrm(ks[12], (F,)), 'wd1': nrm(ks[13], (3, 3, F, F)), 'bd1': nrm(ks[14], (F,)), 'wd2': nrm(ks[15], (3, 3, F, F)), 'bd2': nrm(ks[16], (F,)), 'wd3': nrm(ks[17], (3, 3, F, F)), 'bd3': nrm(ks[18], (F,)), 'wca': nrm(ks[19], (1, 1, F, 3 * C)), 'bca': nrm(ks[20], (3 * C,)), 'wcb': nrm(ks[21], (3, 3, 4 * C, F)), 'bcb': nrm(ks[22], (F,)), 'bn_gamma': jnp.ones((F,), jnp.float32) + nrm(ks[23], (F,)), 'bn_beta': nrm(ks[24], (F,)), 'bn_mean': nrm(ks[25], (F,)), 'bn_var': jnp.ones((F,), jnp.float32) + jax.random.uniform(ks[26], (F,), jnp.float32) * 0.1, 'whf': nrm(ks[27], (1, 1, 3 * C, C)), 'bhf': nrm(ks[28], (C,))}
        return inp
    _L0_conv_all = _L0_conv_setup()
    _L0_conv_in = {k: v for k, v in _L0_conv_all.items() if k in ('w15', 'b15', 'w25', 'b25', 'w13', 'b13', 'w23', 'b23', 'w12', 'b12', 'w22', 'b22', 'wd1', 'bd1', 'wd2', 'bd2', 'wd3', 'bd3', 'wca', 'bca', 'wcb', 'bcb', 'bn_gamma', 'bn_beta', 'bn_mean', 'bn_var', 'whf', 'bhf')}
    del _L0_conv_all

    def _L1_conv_setup():
        import jax, jax.numpy as jnp
        import numpy as np
        key = jax.random.key(seed)
        k1, k2 = jax.random.split(key)
        x = jax.random.normal(k1, (32, 32, 32, 32), dtype=jnp.float32)
        codebook = jax.random.normal(k2, (512, 32), dtype=jnp.float32) * 0.1
        return {'x': x, 'codebook': codebook}
    _L1_conv_all = _L1_conv_setup()
    _L1_conv_in = {k: v for k, v in _L1_conv_all.items() if k in ('codebook',)}
    del _L1_conv_all
    return {'x': x, 'L0_conv_w15': _L0_conv_in['w15'], 'L0_conv_b15': _L0_conv_in['b15'], 'L0_conv_w25': _L0_conv_in['w25'], 'L0_conv_b25': _L0_conv_in['b25'], 'L0_conv_w13': _L0_conv_in['w13'], 'L0_conv_b13': _L0_conv_in['b13'], 'L0_conv_w23': _L0_conv_in['w23'], 'L0_conv_b23': _L0_conv_in['b23'], 'L0_conv_w12': _L0_conv_in['w12'], 'L0_conv_b12': _L0_conv_in['b12'], 'L0_conv_w22': _L0_conv_in['w22'], 'L0_conv_b22': _L0_conv_in['b22'], 'L0_conv_wd1': _L0_conv_in['wd1'], 'L0_conv_bd1': _L0_conv_in['bd1'], 'L0_conv_wd2': _L0_conv_in['wd2'], 'L0_conv_bd2': _L0_conv_in['bd2'], 'L0_conv_wd3': _L0_conv_in['wd3'], 'L0_conv_bd3': _L0_conv_in['bd3'], 'L0_conv_wca': _L0_conv_in['wca'], 'L0_conv_bca': _L0_conv_in['bca'], 'L0_conv_wcb': _L0_conv_in['wcb'], 'L0_conv_bcb': _L0_conv_in['bcb'], 'L0_conv_bn_gamma': _L0_conv_in['bn_gamma'], 'L0_conv_bn_beta': _L0_conv_in['bn_beta'], 'L0_conv_bn_mean': _L0_conv_in['bn_mean'], 'L0_conv_bn_var': _L0_conv_in['bn_var'], 'L0_conv_whf': _L0_conv_in['whf'], 'L0_conv_bhf': _L0_conv_in['bhf'], 'L1_conv_codebook': _L1_conv_in['codebook']}

def reference(x, L0_conv_w15, L0_conv_b15, L0_conv_w25, L0_conv_b25, L0_conv_w13, L0_conv_b13, L0_conv_w23, L0_conv_b23, L0_conv_w12, L0_conv_b12, L0_conv_w22, L0_conv_b22, L0_conv_wd1, L0_conv_bd1, L0_conv_wd2, L0_conv_bd2, L0_conv_wd3, L0_conv_bd3, L0_conv_wca, L0_conv_bca, L0_conv_wcb, L0_conv_bcb, L0_conv_bn_gamma, L0_conv_bn_beta, L0_conv_bn_mean, L0_conv_bn_var, L0_conv_whf, L0_conv_bhf, L1_conv_codebook):
    import jax
    import jax.numpy as jnp

    def _L0_conv_ref(x, w15, b15, w25, b25, w13, b13, w23, b23, w12, b12, w22, b22, wd1, bd1, wd2, bd2, wd3, bd3, wca, bca, wcb, bcb, bn_gamma, bn_beta, bn_mean, bn_var, whf, bhf):
        import jax, jax.numpy as jnp
        import numpy as np
        LEAK = 0.3
        BN_EPS = 0.001

        def _conv(x, w, b, dil=1):
            y = jax.lax.conv_general_dilated(x, w, window_strides=(1, 1), padding='SAME', rhs_dilation=(dil, dil), dimension_numbers=('NHWC', 'HWIO', 'NHWC'))
            return y + b

        def _lrelu(x):
            return jnp.where(x >= 0, x, LEAK * x)

        def _dwt_haar(x):
            a = x[:, ::2, ::2, :]
            b = x[:, ::2, 1::2, :]
            c = x[:, 1::2, ::2, :]
            d = x[:, 1::2, 1::2, :]
            LL = (a + b + c + d) * 0.5
            LH = (c + d - a - b) * 0.5
            HL = (b + d - a - c) * 0.5
            HH = (a - b - c + d) * 0.5
            return (LL, LH, HL, HH)

        def _idwt_haar(LL, LH, HL, HH):
            a = (LL - LH - HL + HH) * 0.5
            b = (LL - LH + HL - HH) * 0.5
            c = (LL + LH - HL - HH) * 0.5
            d = (LL + LH + HL + HH) * 0.5
            B, h, w, C = LL.shape
            top = jnp.stack([a, b], axis=3).reshape(B, h, 2 * w, C)
            bot = jnp.stack([c, d], axis=3).reshape(B, h, 2 * w, C)
            return jnp.stack([top, bot], axis=2).reshape(B, 2 * h, 2 * w, C)
        LL, LH, HL, HH = _dwt_haar(x)
        hf = jnp.concatenate([LH, HL, HH], axis=-1)
        x1 = _lrelu(_conv(_lrelu(_conv(hf, w15, b15)), w25, b25))
        x2 = _lrelu(_conv(_lrelu(_conv(hf, w13, b13)), w23, b23))
        x3 = _lrelu(_conv(_lrelu(_conv(hf, w12, b12)), w22, b22))
        added = x1 + x2 + x3
        y = _lrelu(_conv(added, wd1, bd1, dil=2))
        y = _lrelu(_conv(y, wd2, bd2, dil=2))
        y = _lrelu(_conv(y, wd3, bd3, dil=2))
        alpha = jax.nn.sigmoid(_conv(y, wca, bca))
        phf = alpha * hf
        ll_exp = jnp.concatenate([LL, phf], axis=-1)
        z = _conv(ll_exp, wcb, bcb)
        z = (z - bn_mean) * jax.lax.rsqrt(bn_var + BN_EPS) * bn_gamma + bn_beta
        pLL = z * jax.nn.sigmoid(z)
        phf2 = _conv(phf, whf, bhf)
        return _idwt_haar(pLL, phf2, HL, HH)

    def _L1_conv_ref(x, codebook):
        import jax, jax.numpy as jnp
        import numpy as np
        b, h, w, d = x.shape
        xf = x.reshape(b * h * w, d)
        x_sq = jnp.sum(xf ** 2, axis=1, keepdims=True)
        c_sq = jnp.sum(codebook ** 2, axis=1)
        dot = xf @ codebook.T
        dists = x_sq - 2.0 * dot + c_sq
        idx = jnp.argmin(dists, axis=1)
        vq = codebook[idx]
        return vq.reshape(b, h, w, d)

    def _gn(v, G=32, eps=1e-05):
        B_, H_, W_, C_ = v.shape
        g = v.reshape(B_, H_, W_, G, C_ // G)
        m = jnp.mean(g, axis=(1, 2, 4), keepdims=True)
        s = jnp.var(g, axis=(1, 2, 4), keepdims=True)
        return ((g - m) / jnp.sqrt(s + eps)).reshape(v.shape)

    def _ln_c(v, eps=1e-06):
        m = jnp.mean(v, axis=-1, keepdims=True)
        s = jnp.var(v, axis=-1, keepdims=True)
        return (v - m) / jnp.sqrt(s + eps)

    def _ln_t(v, eps=1e-05):
        m = jnp.mean(v, axis=-1, keepdims=True)
        s = jnp.var(v, axis=-1, keepdims=True)
        return (v - m) / jnp.sqrt(s + eps)

    def _to_tokens(v):
        B_, H_, W_, C_ = v.shape
        return v.reshape(B_, H_ * W_, C_)

    def _from_tokens(t, like):
        return t.reshape(like.shape)
    x = x + _L0_conv_ref(_gn(x), L0_conv_w15, L0_conv_b15, L0_conv_w25, L0_conv_b25, L0_conv_w13, L0_conv_b13, L0_conv_w23, L0_conv_b23, L0_conv_w12, L0_conv_b12, L0_conv_w22, L0_conv_b22, L0_conv_wd1, L0_conv_bd1, L0_conv_wd2, L0_conv_bd2, L0_conv_wd3, L0_conv_bd3, L0_conv_wca, L0_conv_bca, L0_conv_wcb, L0_conv_bcb, L0_conv_bn_gamma, L0_conv_bn_beta, L0_conv_bn_mean, L0_conv_bn_var, L0_conv_whf, L0_conv_bhf)
    x = x + _L1_conv_ref(_gn(x), L1_conv_codebook)
    return x

_drawn_inputs = setup_inputs


def setup_inputs(seed=0):
    import zlib

    import numpy as np

    out = dict(_drawn_inputs(seed))
    spreads = {}
    factors = {'L0_conv_w15': 5.424,
     'L0_conv_b15': 8.0,
     'L0_conv_w25': 5.206,
     'L0_conv_b25': 33.268,
     'L0_conv_w13': 8.0,
     'L0_conv_b13': 8.0,
     'L0_conv_w23': 8.0,
     'L0_conv_b23': 34.042,
     'L0_conv_w12': 8.0,
     'L0_conv_b12': 8.0,
     'L0_conv_w22': 8.0,
     'L0_conv_b22': 38.919,
     'L0_conv_wd1': 4.736,
     'L0_conv_bd1': 64.0,
     'L0_conv_wd2': 3.904,
     'L0_conv_bd2': 200.0,
     'L0_conv_wd3': 3.922,
     'L0_conv_bd3': 200.0,
     'L0_conv_wca': 3.748,
     'L0_conv_bca': 200.0,
     'L0_conv_bcb': 6.033,
     'L0_conv_bn_gamma': 34.486,
     'L0_conv_bn_beta': 4.373,
     'L0_conv_bn_mean': 4.624,
     'L0_conv_bn_var': 200.0,
     'L0_conv_bhf': 3.228}
    for name, (base, spread) in spreads.items():
        noise = np.random.default_rng([zlib.crc32(name.encode()), seed]).standard_normal(out[name].shape)
        drawn = base * np.exp(spread * noise) if base else spread * noise
        out[name] = jnp.asarray(drawn.astype(out[name].dtype))
    for name, factor in factors.items():
        out[name] = (out[name] * factor).astype(out[name].dtype)
    return out
```

```python
import numpy as np
import concourse.bass as bass
from concourse import mybir
from concourse.alu_op_type import AluOpType as ALU
from contextlib import ExitStack

ACT = mybir.ActivationFunctionType
F32 = mybir.dt.float32
BF16 = mybir.dt.bfloat16
U32 = mybir.dt.uint32

P = 128
IMAGES, HEIGHT, WIDTH, CH = 8, 128, 128, 32
CODES = 512
ROWS = HEIGHT // 2
COLS = WIDTH // 2
BLK = 4
JN = COLS // BLK
PAD = 2
RP = ROWS + 2 * PAD
HALF = JN // 2
MAP = JN * ROWS
XCHUNKS = 8
CW = WIDTH // XCHUNKS * CH
QUADS = 2 * JN
LEAK = 0.3
PRIMED = 1
GN_EPS, BN_EPS = 1e-5, 1e-3
LL, HL, LH, HH = range(4)
BANDS = (LH, HL, HH)

CONVS = {
    "w15": (3, (-2, -1, 0, 1, 2), (-2, -1, 0, 1, 2)),
    "w13": (3, (-1, 0, 1), (-1, 0, 1)),
    "w25": (1, (-2, -1, 0, 1, 2), (-2, -1, 0, 1, 2)),
    "w12": (3, (0, 1), (0, 1)),
    "w23": (1, (-1, 0, 1), (-1, 0, 1)),
    "w22": (1, (0, 1), (0, 1)),
    "wd1": (1, (-2, 0, 2), (-2, 0, 2)),
    "wd2": (1, (-2, 0, 2), (-2, 0, 2)),
    "wd3": (1, (-2, 0, 2), (-2, 0, 2)),
    "wca": (3, (0,), (0,)),
    "wcb": (4, (-1, 0, 1), (-1, 0, 1)),
    "whf": (3, (0,), (0,)),
}
ONE_BY_ONE = ("wca", "whf")


def weight_slots():
    slots, first = {}, {}
    for name, (maps, rows, _) in CONVS.items():
        first[name] = len(slots)
        for m in range(maps):
            for kind in range(1 if name in ONE_BY_ONE else 2):
                for ky in range(len(rows)):
                    slots[name, m, kind, ky] = len(slots)
    first["end"] = len(slots)
    return slots, first


SLOTS, FIRST = weight_slots()
NW = FIRST["end"]

ORDER = ["w15", "w13", "w25", "w12", "w23", "w22", "wd1", "wd2", "wd3"]
GROUP = {}
for _n in ORDER:
    for _h in range(2):
        GROUP[_n, _h] = len(GROUP)
for _m in range(3):
    for _h in range(2):
        GROUP["wca", _m, _h] = len(GROUP)
for _n in ("whf", "wcb"):
    for _h in range(2):
        GROUP[_n, _h] = len(GROUP)
NG = len(GROUP)
RING = 4
assert NG % RING == 0

COL = {n: i for i, n in enumerate(["b15", "b13", "b12", "b25", "b23", "b22", "bd1", "bd2", "bd3", "bca0", "bca1",
                                   "bca2", "bcb", "bn_gamma", "bn_beta", "bn_mean", "bn_var", "bhf"])}


def make_plan():
    plan = []
    for n in ORDER:
        maps, rows, _ = CONVS[n]
        for kind in range(2):
            for half in range(2):
                for m in range(maps):
                    for ky in range(len(rows)):
                        plan.append(("mm", n, half, m, kind, ky))
    for m in range(3):
        for half in range(2):
            plan.append(("mm", "wca", half, m, 0, 0))
    lead = 34
    steps = [("mean2",), ("var2",), ("bias2",)]
    steps += [x for q in range(QUADS) for x in ([("ychunk", q // 4)] if q % 4 == 0 else []) + [("quad", q)]]
    at = {}
    gap = (len(plan) - 12 - lead - 10) / QUADS
    at[lead] = steps[0:1]
    at[lead + 4] = steps[1:2]
    at[lead + 8] = steps[2:3]
    rest = steps[3:]
    for q in range(QUADS):
        k = 2 if q % 4 == 0 else 1
        at.setdefault(int(lead + 12 + gap * q), []).extend(rest[:k])
        rest = rest[k:]
    out = []
    for i, x in enumerate(plan):
        out += at.get(i, [])
        out.append(x)
    cb = []
    for m in range(4):
        if m == 3:
            cb += [("mm", "whf", half, 2, 0, 0) for half in range(2)]
        for kind in range(2):
            for half in range(2):
                for ky in range(3):
                    cb.append(("mm", "wcb", half, m, kind, ky))
        if m in (1, 2):
            cb += [("mm", "whf", half, m - 1, 0, 0) for half in range(2)]
        cb.append(("cbmap", m))
    for i, x in enumerate(cb):
        if i % 2 == 0 and i // 2 < XCHUNKS:
            out.append(("xchunk", i // 2))
        if i == 26:
            out.append(("mean1",))
        if i == 30:
            out.append(("var1",))
        out.append(x)
    return out


PLAN = make_plan()
MAKER = {"w25": "w15", "w23": "w13", "w22": "w12", "wd2": "wd1", "wd3": "wd2", "wca": "wd3"}
LEAKY = ORDER
HAS_EDGE = ["w15", "w13", "w12", "wd1", "wd2"]


def last_products():
    seen = {}
    for i, x in enumerate(PLAN):
        if x[0] == "mm":
            key = ("wca", x[3], x[2]) if x[1] == "wca" else (x[1], x[2])
            seen.setdefault(key, []).append(i)
    return {k: (v[0], v[-1]) for k, v in seen.items()}


SPAN = last_products()
MAP_DONE = [max(j for j in range(i) if PLAN[j][0] == "mm") for i, x in enumerate(PLAN) if x[0] == "cbmap"][:3]


EDGES = ((slice(0, P // 2), slice(1, JN), slice(0, JN - 1)),
         (slice(P // 2, P), slice(0, JN - 1), slice(1, JN)))


def wait(eng, sem, value):
    if not isinstance(value, int) or value > 0:
        eng.wait_ge(sem, value)


def wait_apart(eng, sem, value, passed):
    wait(eng, sem, value)
    eng.sem_inc(passed, 1)


def conv_vq_kernel(nc, x, weights, params, codes4, codebook, ident, group_mean, part_mask, out):
    ctx = ExitStack()
    with ctx:
        def sb(name, shape, dt=F32):
            return ctx.enter_context(nc.sbuf_tensor(name, shape, dt))

        def sem(name):
            return ctx.enter_context(nc.semaphore(name))

        w_sb = sb("w_sb", [P, NW, P])
        prm = sb("prm", [P, len(COL)])
        idn = sb("idn", [P, P])
        gmean = sb("gmean", [P, P])
        pmask = sb("pmask", [P, 4])
        cb4 = sb("cb4", [P, CODES])
        cbsq = sb("cbsq", [CH, CODES])
        cbs = sb("cbs", [P, CODES])
        negones = sb("negones", [CH, P])
        negmean = sb("negmean", [CH, P])
        ones3 = sb("ones3", [P, P], BF16)
        bparts = sb("bparts", [P, CODES], BF16)
        btmp = sb("btmp", [P, CODES], BF16)
        brest = sb("brest", [P, CODES])
        xnat = sb("xnat", [P, 2, CW])
        xord = sb("xord", [P, 2, CW])
        xt = sb("xt", [P, 2, 2, 2, 2, ROWS])
        sd = sb("sd", [P, 2, 2, 2, ROWS])
        bands = [sb(f"bands{i}", [P, 2, JN, 2, ROWS]) for i in range(2)]
        hf = [[sb(f"hf{m}{k}", [P, JN, RP]) for k in range(2)] for m in range(3)]
        lln = [sb(f"lln{k}", [P, JN, RP]) for k in range(2)]
        ha = [sb(f"ha{k}", [P, JN, RP]) for k in range(2)]
        hb = [sb(f"hb{k}", [P, JN, RP]) for k in range(2)]
        br = [sb(f"br{m}", [P, JN, ROWS]) for m in range(3)]
        wtmp = sb("wtmp", [P, 2, JN // 4, 2, ROWS])
        z = sb("z", [P, 2, HALF, ROWS])
        ync = sb("ync", [P, 2, CW])
        vqc = sb("vqc", [P, 2, CW])
        idx = sb("idx", [P, 2, 16, 8], U32)
        top8 = sb("top8", [P, 4, 8])
        st1 = sb("st1", [P, XCHUNKS, 6])
        st2 = sb("st2", [P, XCHUNKS, 6])
        mv = [sb(f"mv{i}", [P, 2]) for i in range(2)]
        mall = [sb(f"mall{i}", [P, 1]) for i in range(2)]
        dev = [sb(f"dev{i}", [P, 1]) for i in range(2)]
        vsum = [sb(f"vsum{i}", [P, 1]) for i in range(2)]
        veps = [sb(f"veps{i}", [P, 1]) for i in range(2)]
        rstd = [sb(f"rstd{i}", [P, 1]) for i in range(2)]
        scale1 = sb("scale1", [P, 1])
        shift1 = sb("shift1", [P, 1])
        resid = [sb(f"resid{i}", [P, 1]) for i in range(2)]
        scale2 = sb("scale2", [P, 1])
        power = sb("power", [P, 1])
        bnv = sb("bnv", [P, 1])
        bnr = sb("bnr", [P, 1])
        bns = sb("bns", [P, 1])
        bnt = sb("bnt", [P, 1])
        bnb = sb("bnb", [P, 1])
        bnsh = sb("bnsh", [P, 1])
        bnbh = sb("bnbh", [P, 1])
        bhfh = sb("bhfh", [P, 1])

        ring = [ctx.enter_context(nc.psum_tensor(f"ring{i}", [P, HALF, ROWS], F32)) for i in range(RING)]
        score = [ctx.enter_context(nc.psum_tensor(f"score{i}", [P, CODES], F32)) for i in range(4)]

        s_w = {n: sem(f"s_w_{n}") for n in CONVS}
        s_const = sem("s_const")
        s_zero = sem("s_zero")
        s_init = sem("s_init")
        s_x = [sem(f"s_x{i}") for i in range(2)]
        s_xT = sem("s_xT")
        s_xord = sem("s_xord")
        s_xev = sem("s_xev")
        s_dwt = sem("s_dwt")
        s_agg = [sem(f"s_agg{i}") for i in range(2)]
        s_mean = [sem(f"s_mean{i}") for i in range(2)]
        s_dev = [sem(f"s_dev{i}") for i in range(2)]
        s_var = [sem(f"s_var{i}") for i in range(2)]
        s_veps = [sem(f"s_veps{i}") for i in range(2)]
        s_rstd = [sem(f"s_rstd{i}") for i in range(2)]
        s_norm = sem("s_norm")
        s_lln = sem("s_lln")
        s_hfw = sem("s_hfw")
        s_grp = sem("s_grp")
        s_free = sem("s_free")
        s_leaky = sem("s_leaky")
        s_edge = sem("s_edge")
        s_sum = sem("s_sum")
        s_phf = sem("s_phf")
        s_pedge = sem("s_pedge")
        s_cbmap = sem("s_cbmap")
        s_band = sem("s_band")
        s_neg = sem("s_neg")
        s_cbs = sem("s_cbs")
        s_bias = sem("s_bias")
        s_parts = sem("s_parts")
        s_quad = sem("s_quad")
        s_idx = sem("s_idx")
        s_yT = sem("s_yT")
        s_yev = sem("s_yev")
        s_gather = [sem(f"s_gather{i}") for i in range(2)]
        s_add = sem("s_add")
        s_store = [sem(f"s_store{i}") for i in range(2)]
        s_yedge = sem("s_yedge")
        s_bnv = sem("s_bnv")
        s_bnr = sem("s_bnr")
        s_bn = sem("s_bn")
        s_passed = [sem(f"s_passed{i}") for i in range(2)]
        s_top = sem("s_top")
        s_d0, s_dn, s_dc, s_dq = (sem(n) for n in ("s_d0", "s_dn", "s_dc", "s_dq"))

        LEAKY_TILE = {"w15": ha, "w13": hb, "w12": ha, "wd1": ha, "wd2": hb, "wd3": ha}

        block = ctx.enter_context(nc.Block())
        xv = x.rearrange("b (i e) w c -> b e i (w c)", e=2)
        ov = out.rearrange("b (i e) w c -> b e i (w c)", e=2)

        def rounds(eng, body):
            body(0, 0, True, False, True)
            with eng.Fori(0, (IMAGES - 2) // 2) as i:
                body(2 * i + 1, 1, True, True, True)
                body(2 * i + 2, 0, True, True, True)
            body(IMAGES - 1, 1, True, True, False)
            body(IMAGES, 0, False, True, False)

        def own(tile, half, rows=slice(PAD, PAD + ROWS)):
            return tile[:, half * HALF:(half + 1) * HALF, rows]

        def raw(par, slot):
            return bands[par][:, slot // 2, :, slot % 2, :]

        @block.sync
        def _(sp):
            def load(b, k):
                wait(sp, s_xord, XCHUNKS * b + k - 1)
                for e in range(2):
                    sp.dma_start(xnat[e * ROWS:(e + 1) * ROWS, k % 2, :],
                                 xv[b, e, :, k * CW:(k + 1) * CW] if isinstance(b, int) else
                                 xv[bass.ds(b, 1), e, :, k * CW:(k + 1) * CW].rearrange("b i n -> (b i) n")
                                 ).then_inc(s_x[k % 2], 16)

            def store(v, c):
                sp.wait_ge(s_add, PRIMED + XCHUNKS * v + c + 1)
                for e in range(2):
                    sp.dma_start(ov[v, e, :, c * CW:(c + 1) * CW] if isinstance(v, int) else
                                 ov[bass.ds(v, 1), e, :, c * CW:(c + 1) * CW].rearrange("b i n -> (b i) n"),
                                 vqc[e * ROWS:(e + 1) * ROWS, c % 2, :]).then_inc(s_store[c % 2], 16)

            for dst, src in ((idn, ident), (gmean, group_mean), (prm, params), (cb4, codes4), (pmask, part_mask)):
                sp.dma_start(dst[:, :], src[:, :]).then_inc(s_const, 16)
            for k in range(XCHUNKS):
                load(0, k)

            def body(b, par, conv, quant, nxt):
                if nxt:
                    for k in range(2):
                        load(b + 1, k)
                if quant:
                    for c in range(XCHUNKS - 1):
                        store(b - 1, c)
                if nxt:
                    for k in range(2, XCHUNKS):
                        load(b + 1, k)
                if quant:
                    store(b - 1, XCHUNKS - 1)

            rounds(sp, body)
            for i in range(2):
                sp.wait_ge(s_store[i], PRIMED + 32 * (XCHUNKS // 2) * IMAGES)

        @block.tensor
        def _(pe):
            def transpose4(dst, src, last):
                for n in range(4):
                    t = nc.tensor.transpose(dst[:, n * P:(n + 1) * P], src(n), idn[:, :])
                t.then_inc(last, 1)

            def xchunk(b, k):
                pe.wait_ge(s_xord, XCHUNKS * b + k + 1)
                if k == 0:
                    wait(pe, s_veps[0], b)
                if k >= 4:
                    pe.wait_ge(s_xev, XCHUNKS * b + k - 3)
                else:
                    wait(pe, s_idx, 4 * QUADS * (b - 1))
                transpose4(score[k % 4], lambda n: xord[:, k % 2, n * P:(n + 1) * P], s_xT)

            def combine(which, src, col, ready, n, done):
                pe.wait_ge(ready, n + 1)
                nc.tensor.matmul(score[col][:, 0:1], gmean[:, :], src, start=True, stop=True).then_inc(done, 1)

            def mean(which, n):
                if which == 0:
                    pe.wait_ge(s_xev, XCHUNKS * (n + 1))
                combine(which, mv[which][:, 0:1], 0, s_agg[which], n, s_mean[which])

            def var(which, n):
                combine(which, vsum[which][:, :], 1, s_dev[which], n, s_var[which])

            def bias2(v):
                pe.wait_ge(s_neg, v + 1)
                pe.wait_ge(s_cbs, v + 1)
                nc.tensor.matmul(score[2][:, :], negmean[:, :], cbs[0:CH, :], start=True, stop=False)
                nc.tensor.matmul(score[2][:, :], negones[:, :], cbsq[:, :], start=False, stop=True)\
                    .then_inc(s_bias, 1)

            def yview(par, wp, j):
                return bands[par][:, wp, j].rearrange("p e i -> p (e i)")

            def ychunk(v, par, c):
                if c:
                    pe.wait_ge(s_idx, 4 * QUADS * v + 16 * c - 3)
                else:
                    pe.wait_ge(s_parts, v + 1)
                transpose4(score[0], lambda n: yview(par, n % 2, 2 * c + n // 2), s_yT)

            def quad(v, par, q):
                if q:
                    pe.wait_ge(s_idx, 4 * QUADS * v + 4 * q)
                if q % 4 == 0:
                    pe.wait_ge(s_yev, XCHUNKS * v + q // 4 + 1)
                j, wp = q // 2, q % 2
                for g in range(4):
                    lo = 32 * g
                    nc.tensor.matmul(score[g][:, :], ones3[lo:lo + 3, :], bparts[lo:lo + 3, :],
                                     start=True, stop=False)
                for g in range(4):
                    lo = 32 * g
                    t = nc.tensor.matmul(score[g][:, :], yview(par, wp, j)[lo:lo + 32, :],
                                         cbs[lo:lo + 32, :], start=False, stop=True)
                t.then_inc(s_quad, 1)

            def sources(n, m):
                if n in ("w15", "w13", "w12"):
                    return hf[m]
                if n == "wcb":
                    return lln if m == 0 else hf[m - 1]
                if n == "whf":
                    return hf[m]
                return {"w25": ha, "w23": hb, "w22": ha, "wd1": hb, "wd2": ha, "wd3": hb, "wca": ha}[n]

            def inputs_ready(b, n, half, m, kind, new):
                if n == "w15" and half == 0:
                    pe.wait_ge(s_hfw, 6 * b + (m + 1 if kind == 0 else m + 4))
                elif n in MAKER and m == 0:
                    if kind == 0:
                        pe.wait_ge(s_leaky, len(LEAKY) * 2 * b + GROUP[MAKER[n], half] + 1)
                    elif half == 0:
                        pe.wait_ge(s_edge, len(HAS_EDGE) * b + HAS_EDGE.index(MAKER[n]) + 1)
                elif n == "wd1":
                    if kind == 0:
                        pe.wait_ge(s_sum, 2 * b + half + 1)
                    elif half == 0:
                        pe.wait_ge(s_yedge, b + 1)
                elif n == "wcb":
                    if m == 0:
                        if half == 0 and kind == 0:
                            pe.wait_ge(s_lln, b + 1)
                    elif kind == 0:
                        pe.wait_ge(s_phf, 6 * b + 2 * (m - 1) + half + 1)
                    elif half == 0:
                        pe.wait_ge(s_pedge, 3 * b + m)
                elif n == "whf" and m == 2:
                    pe.wait_ge(s_phf, 6 * b + 2 * m + half + 1)

            def product(i, b, n, half, m, kind, ky, seen):
                key = ("wca", m, half) if n == "wca" else (n, half)
                first, last = SPAN[key]
                g = GROUP[key]
                if i == first:
                    wait(pe, s_free, NG * b + g - (RING - 1))
                if (n, half, m, kind) not in seen:
                    seen.add((n, half, m, kind))
                    if isinstance(b, int) and b == 0 and ("w", n) not in seen:
                        seen.add(("w", n))
                        pe.wait_ge(s_w[n], 16)
                    inputs_ready(b, n, half, m, kind, seen)
                di = CONVS[n][1][ky]
                t = nc.tensor.matmul(ring[g % RING][:, :, :], w_sb[:, SLOTS[n, m, kind, ky], :],
                                     own(sources(n, m)[kind], half, slice(PAD + di, PAD + di + ROWS)),
                                     start=(i == first), stop=(i == last))
                if i == last:
                    t.then_inc(s_grp, 1)
                elif i in MAP_DONE:
                    t.then_inc(s_cbmap, 1)

            def body(b, par, conv, quant, nxt):
                seen, v = set(), b - 1
                for i, step in enumerate(PLAN):
                    what = step[0]
                    if what == "mm" and conv:
                        product(i, b, *step[1:], seen)
                    elif quant and what == "mean2":
                        mean(1, v)
                    elif quant and what == "var2":
                        var(1, v)
                    elif quant and what == "bias2":
                        bias2(v)
                    elif quant and what == "ychunk":
                        ychunk(v, 1 - par, step[1])
                    elif quant and what == "quad":
                        quad(v, 1 - par, step[1])
                    elif nxt and what == "xchunk":
                        xchunk(b + 1, step[1])
                    elif nxt and what == "mean1":
                        mean(0, b + 1)
                    elif nxt and what == "var1":
                        var(0, b + 1)

            pe.wait_ge(s_const, 16 * 5)
            pe.wait_ge(s_init, 1)
            for k in range(XCHUNKS):
                xchunk(0, k)
            mean(0, 0)
            var(0, 0)
            rounds(pe, body)

        @block.scalar
        def _(act):
            for n in CONVS:
                hi = min([f for f in FIRST.values() if f > FIRST[n]])
                act.dma_start(w_sb[:, FIRST[n]:hi, :], weights[:, FIRST[n]:hi, :]).then_inc(s_w[n], 16)

            def col(name):
                return prm[:, COL[name]:COL[name] + 1]

            def edge_copy(tiles):
                for p, src, dst in EDGES:
                    t = nc.scalar.copy(tiles[1][p, dst, PAD:PAD + ROWS], tiles[0][p, src, PAD:PAD + ROWS])
                return t

            def evacuate(b, key):
                g = GROUP[key]
                n, half = key[0], key[-1]
                bank = ring[g % RING]
                act.wait_ge(s_grp, NG * b + g + 1)
                if n in LEAKY:
                    wait(act, s_leaky, len(LEAKY) * 2 * b + g - 1)
                    nc.scalar.activation(z[:, g % 2], bank[:, :, :], ACT.Identity, bias=col("b" + n[1:]))\
                        .then_inc(s_free, 1)
                    if half == 1 and n in HAS_EDGE:
                        act.wait_ge(s_leaky, len(LEAKY) * 2 * b + g + 1)
                        edge_copy(LEAKY_TILE[n]).then_inc(s_edge, 1)
                    if half == 1 and n == "w22":
                        act.wait_ge(s_sum, 2 * b + 2)
                        edge_copy(hb).then_inc(s_yedge, 1)
                elif n == "wca":
                    m = key[1]
                    t = nc.scalar.activation(br[m][:, half * HALF:(half + 1) * HALF, :], bank[:, :, :],
                                             ACT.Sigmoid, bias=col(f"bca{m}"))
                    t.then_inc(s_free, 1)
                    if m == 2 and half == 1:
                        for k in range(3):
                            act.wait_ge(s_phf, 6 * b + 2 * k + 2)
                            edge_copy(hf[k]).then_inc(s_pedge, 1)
                elif n == "whf":
                    t = nc.scalar.activation(br[2][:, half * HALF:(half + 1) * HALF, :], bank[:, :, :],
                                             ACT.Identity, bias=bhfh[:, :], scale=0.5)
                    t.then_inc(s_free, 1)
                else:
                    nc.scalar.activation(br[0][:, half * HALF:(half + 1) * HALF, :], bank[:, :, :],
                                         ACT.Identity, bias=bnbh[:, :], scale=bnsh[:, :])
                    t = nc.scalar.activation(br[1][:, half * HALF:(half + 1) * HALF, :], bank[:, :, :],
                                             ACT.Sigmoid, bias=bnb[:, :], scale=bns[:, :])
                    t.then_inc(s_free, 1)

            def xorder(b, k):
                act.wait_ge(s_x[k % 2], 32 * ((XCHUNKS // 2) * b + k // 2 + 1))
                wait(act, s_xT, XCHUNKS * b + k - 1)
                src = xnat[:, k % 2, :].rearrange("p (j g w c) -> p w j g c", g=4, w=2, c=CH)
                dst = xord[:, k % 2, :].rearrange("p (w j g c) -> p w j g c", w=2, g=4, c=CH)
                for w in range(2):
                    t = nc.scalar.copy(dst[:, w], src[:, w])
                t.then_inc(s_xord, 1)

            def xcopy(b, k):
                if k + 2 < XCHUNKS:
                    xorder(b, k + 2)
                act.wait_ge(s_xT, XCHUNKS * b + k + 1)
                wait(act, s_dwt, XCHUNKS * b + k - 1)
                nc.scalar.copy(xt[:, k % 2].rearrange("p w j e i -> p (w j e i)"), score[k % 4][:, :])\
                    .then_inc(s_xev, 1)

            def ycopy(v, c):
                act.wait_ge(s_yT, XCHUNKS * v + c + 1)
                act.wait_ge(s_add, PRIMED + XCHUNKS * v + max(c - 1, 0))
                dst = ync[:, c % 2, :].rearrange("p (j g w c) -> p j w g c", g=4, w=2, c=CH)
                src = score[0][:, :].rearrange("p (j w g c) -> p j w g c", g=4, w=2, c=CH)
                for j in range(2):
                    t = nc.scalar.copy(dst[:, j], src[:, j])
                t.then_inc(s_yev, 1)

            def normal_ll(n, par):
                act.wait_ge(s_norm, n + 1)
                wait(act, s_cbmap, 3 * (n - 1) + 1)
                src = raw(par, LL)
                nc.scalar.activation(lln[0][:, :, PAD:PAD + ROWS], src, ACT.Identity, bias=shift1[:, :],
                                     scale=scale1[:, :])
                for p, s, d in EDGES:
                    t = nc.scalar.activation(lln[1][p, d, PAD:PAD + ROWS], src[p, s], ACT.Identity,
                                             bias=shift1[p, :], scale=scale1[p, :])
                t.then_inc(s_lln, 1)

            def normal_own(n, par, m):
                if m < 2:
                    wait(act, s_cbmap, 3 * (n - 1) + m + 2)
                else:
                    wait(act, s_grp, NG * n)
                nc.scalar.activation(hf[m][0][:, :, PAD:PAD + ROWS], raw(par, BANDS[m]), ACT.Identity,
                                     bias=0.0, scale=scale1[:, :]).then_inc(s_hfw, 1)

            def normal_edge(n, par, m):
                for p, s, d in EDGES:
                    t = nc.scalar.activation(hf[m][1][p, d, PAD:PAD + ROWS], raw(par, BANDS[m])[p, s],
                                             ACT.Identity, bias=0.0, scale=scale1[p, :])
                t.then_inc(s_hfw, 1)

            def body(b, par, conv, quant, nxt):
                v = b - 1
                for i, step in enumerate(PLAN):
                    what = step[0]
                    if nxt and i == 0:
                        for k in range(2):
                            xorder(b + 1, k)
                    if quant and what == "ychunk":
                        ycopy(v, step[1])
                    elif nxt and what == "xchunk":
                        xcopy(b + 1, step[1])
                    elif nxt and what == "cbmap" and step[1] == 2:
                        normal_ll(b + 1, 1 - par)
                        normal_own(b + 1, 1 - par, 0)
                        normal_own(b + 1, 1 - par, 1)
                    elif conv and what == "mm":
                        for key, (_, last) in SPAN.items():
                            if last == i:
                                evacuate(b, key)
                if nxt:
                    normal_own(b + 1, 1 - par, 2)
                    for m in range(3):
                        normal_edge(b + 1, 1 - par, m)

            act.wait_ge(s_zero, 1)
            act.wait_ge(s_bn, 1)
            for k in range(2):
                xorder(0, k)
            for k in range(XCHUNKS):
                xcopy(0, k)
            normal_ll(0, 0)
            for m in range(3):
                normal_own(0, 0, m)
            for m in range(3):
                normal_edge(0, 0, m)
            rounds(act, body)

        @block.vector
        def _(dve):
            def after(ins, sem, value):
                ins.then_inc(sem, 1)
                dve.wait_ge(sem, value)

            def statistics(which, n, sem, base):
                dve.wait_ge(s_mean[which], n + 1)
                after(nc.vector.tensor_copy(mall[which][:, :], score[0][:, 0:1]), sem, base + 1)
                after(nc.vector.tensor_tensor(dev[which][:, :], mv[which][:, 0:1], mall[which][:, :],
                                              ALU.subtract), sem, base + 2)
                nc.vector.scalar_tensor_tensor(out=vsum[which][:, :], in0=dev[which][:, :],
                                               scalar=dev[which][:, :], in1=mv[which][:, 1:2], op0=ALU.mult,
                                               op1=ALU.add).then_inc(s_dev[which], 1)

            def variance(which, n):
                dve.wait_ge(s_var[which], n + 1)
                nc.vector.tensor_scalar_add(veps[which][:, :], score[1][:, 0:1], GN_EPS).then_inc(s_veps[which], 1)
                dve.wait_ge(s_rstd[which], n + 1)

            NSTEP = 2 * XCHUNKS + 4

            def xchunk(n, par, k):
                base = NSTEP * n + 2 * k
                dve.wait_ge(s_xev, XCHUNKS * n + k + 1)
                slot = xt[:, k % 2]
                nc.vector.bn_stats(st1[:, k, :], slot.rearrange("p w j e i -> p (w j e i)"))
                wait(dve, s_dwt, XCHUNKS * n + k)
                nc.vector.tensor_tensor(sd[:, 0], slot[:, 0], slot[:, 1], ALU.add).then_inc(s_dn, 1)
                nc.vector.tensor_tensor(sd[:, 1], slot[:, 1], slot[:, 0], ALU.subtract).then_inc(s_dn, 1)
                dve.wait_ge(s_dn, base + 2)
                js = slice(2 * k, 2 * k + 2)
                pair = sd[:, :].rearrange("p s j e i -> p e j s i")
                nc.vector.tensor_tensor(bands[par][:, 0, js], pair[:, 0], pair[:, 1], ALU.add)
                nc.vector.tensor_tensor(bands[par][:, 1, js], pair[:, 1], pair[:, 0], ALU.subtract)\
                    .then_inc(s_dwt, 1)

            def aggregate1(n):
                wait_apart(dve, s_dwt, XCHUNKS * (n + 1), s_passed[0])
                nc.vector.bn_aggr(mv[0][:, :], st1[:, :, :]).then_inc(s_agg[0], 1)

            def mean1(n):
                statistics(0, n, s_dn, NSTEP * n + 2 * XCHUNKS)

            def var1(n, par):
                variance(0, n)
                wait(dve, s_hfw, 6 * n)
                nc.vector.tensor_scalar_mul(scale1[:, :], rstd[0][:, :], 0.5).then_inc(s_dn, 1)
                nc.vector.tensor_scalar(resid[par][:, :], rstd[0][:, :], 0.25, 0.25, ALU.mult, ALU.add)\
                    .then_inc(s_dn, 1)
                dve.wait_ge(s_dn, NSTEP * (n + 1))
                nc.vector.tensor_scalar(shift1[:, :], mall[0][:, :], rstd[0][:, :], -2.0, ALU.mult, ALU.mult)\
                    .then_inc(s_norm, 1)

            def leaky(b, n, half):
                g = GROUP[n, half]
                js = slice(half * HALF, (half + 1) * HALF)
                dst = own(LEAKY_TILE[n][0], half) if n in LEAKY_TILE else br[("w25", "w23", "w22").index(n)][:, js, :]
                dve.wait_ge(s_free, NG * b + g + 1)
                nc.vector.scalar_tensor_tensor(out=dst, in0=z[:, g % 2], scalar=LEAK, in1=z[:, g % 2],
                                               op0=ALU.mult, op1=ALU.max).then_inc(s_leaky, 1)

            def branch_sum(b, half):
                js = slice(half * HALF, (half + 1) * HALF)
                dve.wait_ge(s_leaky, len(LEAKY) * 2 * b + GROUP["w22", half] + 1)
                after(nc.vector.tensor_tensor(br[0][:, js, :], br[0][:, js, :], br[1][:, js, :], ALU.add),
                      s_dc, 2 * b + half + 1)
                nc.vector.tensor_tensor(own(hb[0], half), br[0][:, js, :], br[2][:, js, :], ALU.add)\
                    .then_inc(s_sum, 1)

            QSTEP = 1 + 3 + 4 * 4 + 1 + 2 + 4

            def finish(v, par):
                bn = bands[par]
                part = wtmp[:, :].rearrange("p e j s i -> p s j e i")
                base = QSTEP * v
                dve.wait_ge(s_free, NG * (v + 1))
                after(nc.vector.tensor_tensor(br[0][:, :, :], br[0][:, :, :], br[1][:, :, :], ALU.mult),
                      s_dq, base + 1)
                dve.wait_ge(s_hfw, 6 * v + 6)
                nc.vector.scalar_tensor_tensor(out=raw(par, LL), in0=raw(par, LL), scalar=0.25, in1=br[0][:, :, :],
                                               op0=ALU.mult, op1=ALU.add).then_inc(s_dq, 1)
                nc.vector.tensor_scalar(bn[:, :, :, 1], bn[:, :, :, 1], resid[par][:, :], None, ALU.mult)\
                    .then_inc(s_dq, 1)
                nc.vector.scalar_tensor_tensor(out=raw(par, LH), in0=raw(par, LH), scalar=0.25, in1=br[2][:, :, :],
                                               op0=ALU.mult, op1=ALU.add).then_inc(s_band, 1)
                dve.wait_ge(s_dq, base + 3)
                dve.wait_ge(s_band, v + 1)
                for r in range(4):
                    js = slice(r * JN // 4, (r + 1) * JN // 4)
                    at = base + 4 + 4 * r
                    nc.vector.tensor_tensor(wtmp[:, 0], bn[:, 0, js], bn[:, 1, js], ALU.subtract)\
                        .then_inc(s_dq, 1)
                    nc.vector.tensor_tensor(wtmp[:, 1], bn[:, 0, js], bn[:, 1, js], ALU.add)\
                        .then_inc(s_dq, 1)
                    dve.wait_ge(s_dq, at + 1)
                    nc.vector.tensor_tensor(bn[:, 0, js], part[:, 0], part[:, 1], ALU.subtract)\
                        .then_inc(s_dq, 1)
                    nc.vector.tensor_tensor(bn[:, 1, js], part[:, 0], part[:, 1], ALU.add)\
                        .then_inc(s_dq, 1)
                    dve.wait_ge(s_dq, at + 3)
                flat = bn[:, :].rearrange("p w j e i -> p (w j e i)")
                for k in range(8):
                    t = nc.vector.bn_stats(st2[:, k, :], flat[:, k * 512:(k + 1) * 512])
                t.then_inc(s_dq, 1)
                wait_apart(dve, s_dq, base + 20, s_passed[0])
                nc.vector.bn_aggr(mv[1][:, :], st2[:, :, :]).then_inc(s_agg[1], 1)

            def var2(v):
                variance(1, v)
                base = QSTEP * v + 22
                after(nc.vector.tensor_scalar_mul(scale2[:, :], rstd[1][:, :], 2.0), s_dq, base + 1)
                nc.vector.tensor_scalar(negmean[:, :], negones[:, :], mall[1][0:CH, :], None, ALU.mult)\
                    .then_inc(s_neg, 1)
                nc.vector.tensor_scalar(cbs[:, :], cb4[:, :], scale2[:, :], None, ALU.mult).then_inc(s_cbs, 1)

            def bias2(v):
                base = QSTEP * v + 23
                dve.wait_ge(s_bias, v + 1)
                after(nc.vector.tensor_copy(btmp[:, :], score[2][:, :]), s_dq, base + 1)
                after(nc.vector.scalar_tensor_tensor(out=brest[:, :], in0=btmp[:, :], scalar=pmask[:, 0:1],
                                                     in1=score[2][:, :], op0=ALU.mult, op1=ALU.add), s_dq, base + 2)
                after(nc.vector.tensor_copy(btmp[:, :], brest[:, :]), s_dq, base + 3)
                after(nc.vector.scalar_tensor_tensor(out=brest[:, :], in0=btmp[:, :], scalar=pmask[:, 1:2],
                                                     in1=brest[:, :], op0=ALU.mult, op1=ALU.add), s_dq, base + 4)
                nc.vector.tensor_copy(bparts[:, :], brest[:, :]).then_inc(s_parts, 1)

            def quad(v, q):
                c = q // 4
                if q % 4 == 0:
                    dve.wait_ge(s_add, PRIMED + XCHUNKS * v + max(c - 1, 0))
                wait_apart(dve, s_quad, QUADS * v + q + 1, s_passed[0])

                for g in range(4):
                    t = nc.vector.max(top8[:, g, :], score[g][:, :])
                t.then_inc(s_top, 1)
                wait_apart(dve, s_top, QUADS * v + q + 1, s_passed[0])
                for g in range(4):
                    nc.vector.max_index(idx[:, c % 2, 4 * (q % 4) + g, :], top8[:, g, :], score[g][:, :])\
                        .then_inc(s_idx, 1)

            def body(b, par, conv, quant, nxt):
                v = b - 1
                if quant:
                    finish(v, 1 - par)
                for i, step in enumerate(PLAN):
                    what = step[0]
                    if quant and what == "mean2":
                        statistics(1, v, s_dq, QSTEP * v + 20)
                    elif quant and what == "var2":
                        var2(v)
                    elif quant and what == "bias2":
                        bias2(v)
                    elif quant and what == "quad":
                        quad(v, step[1])
                    elif nxt and what == "xchunk":
                        xchunk(b + 1, 1 - par, step[1])
                        if step[1] == XCHUNKS - 1:
                            aggregate1(b + 1)
                    elif nxt and what == "mean1":
                        mean1(b + 1)
                    elif nxt and what == "var1":
                        var1(b + 1, 1 - par)
                    elif conv and what == "mm":
                        n, half = step[1], step[2]
                        if n in LEAKY and SPAN[n, half][1] == i:
                            leaky(b, n, half)
                            if n == "w22":
                                branch_sum(b, half)

            nc.vector.memset(negones[:, :], -1.0)
            nc.vector.memset(ones3[:, :], 1.0).then_inc(s_init, 1)
            dve.wait_ge(s_const, 16 * 5)
            after(nc.vector.tensor_tensor(cbsq[:, :], cb4[0:CH, :], cb4[0:CH, :], ALU.mult), s_d0, 1)

            def col(name):
                return prm[:, COL[name]:COL[name] + 1]

            nc.vector.tensor_scalar_add(bnv[:, :], col("bn_var"), BN_EPS).then_inc(s_bnv, 1)
            dve.wait_ge(s_bnr, 1)
            after(nc.vector.tensor_tensor(bns[:, :], bnr[:, :], col("bn_gamma"), ALU.mult), s_d0, 2)
            after(nc.vector.tensor_tensor(bnt[:, :], col("bcb"), col("bn_mean"), ALU.subtract), s_d0, 3)
            after(nc.vector.scalar_tensor_tensor(out=bnb[:, :], in0=bnt[:, :], scalar=bns[:, :],
                                                 in1=col("bn_beta"), op0=ALU.mult, op1=ALU.add), s_d0, 4)
            nc.vector.tensor_scalar_mul(bnsh[:, :], bns[:, :], 0.5)
            nc.vector.tensor_scalar_mul(bnbh[:, :], bnb[:, :], 0.5)
            nc.vector.tensor_scalar_mul(bhfh[:, :], col("bhf"), 0.5).then_inc(s_bn, 1)
            for k in range(XCHUNKS):
                xchunk(0, 0, k)
            aggregate1(0)
            mean1(0)
            var1(0, 0)
            rounds(dve, body)

        @block.gpsimd
        def _(pool):
            def rsqrt(dst, src, done):
                nc.gpsimd.tensor_tensor(dst[:, :], src[:, :], power[:, :], ALU.pow).then_inc(done, 1)

            def norm(which, n):
                pool.wait_ge(s_veps[which], n + 1)
                rsqrt(rstd[which], veps[which], s_rstd[which])

            def gathers(v, q):
                c = q // 4
                if q % 4 == 0:
                    pool.wait_ge(s_store[c % 2], PRIMED + 32 * ((XCHUNKS // 2) * v + c // 2))
                for g in range(4):
                    wait_apart(pool, s_idx, 4 * (QUADS * v + q) + g + 1, s_passed[1])
                    w = 8 * (q % 4 // 2) + 2 * g + q % 2
                    nc.gpsimd.indirect_dma_start(
                        vqc[:, c % 2, w * CH:(w + 1) * CH], None, codebook[:, :],
                        bass.IndirectOffsetOnAxis(idx[:, c % 2, 4 * (q % 4) + g, 0:1], 0))\
                        .then_inc(s_gather[c % 2], 16)

            def add(v, c):
                pool.wait_ge(s_yev, XCHUNKS * v + c + 1)
                pool.wait_ge(s_gather[c % 2], 256 * ((XCHUNKS // 2) * v + c // 2 + 1))
                nc.gpsimd.tensor_tensor(vqc[:, c % 2, :], vqc[:, c % 2, :], ync[:, c % 2, :], ALU.add)\
                    .then_inc(s_add, 1)

            def attend(b, m):
                for half in range(2):
                    js = slice(half * HALF, (half + 1) * HALF)
                    pool.wait_ge(s_free, NG * b + GROUP["wca", m, half] + 1)
                    nc.gpsimd.tensor_tensor(own(hf[m][0], half), own(hf[m][0], half), br[m][:, js, :], ALU.mult)\
                        .then_inc(s_phf, 1)

            def body(b, par, conv, quant, nxt):
                v = b - 1
                for i, step in enumerate(PLAN):
                    what = step[0]
                    if quant and what == "var2":
                        norm(1, v)
                    elif quant and what == "quad":
                        gathers(v, step[1])
                        if step[1] % 4 == 1 and step[1] > 4:
                            add(v, step[1] // 4 - 1)
                    elif nxt and what == "var1":
                        norm(0, b + 1)
                    elif conv and what == "mm":
                        for m in range(3):
                            if SPAN["wca", m, 1][1] == i:
                                attend(b, m)
                        if quant and SPAN["wca", 2, 1][1] == i:
                            add(v, XCHUNKS - 1)
                if quant and not conv:
                    add(v, XCHUNKS - 1)

            for counter in (s_add, *s_store):
                pool.sem_inc(counter, PRIMED)
            nc.gpsimd.memset(power[:, :], -0.5)
            tiles = [t for pair in (*hf, lln, ha, hb) for t in pair]
            for t in tiles:
                last = nc.gpsimd.memset(t[:, :, :], 0.0)
            last.then_inc(s_zero, 1)
            pool.wait_ge(s_zero, 1)
            pool.wait_ge(s_bnv, 1)
            rsqrt(bnr, bnv, s_bnr)
            norm(0, 0)
            rounds(pool, body)

    return nc



def block_matrices(w, name):
    maps, rows, cols = CONVS[name]
    n = FIRST[name]
    out = np.zeros((BLK, CH, len([k for k in SLOTS if k[0] == name]), BLK, CH), w.dtype)
    for (conv, m, kind, ky), slot in SLOTS.items():
        if conv != name:
            continue
        for g in range(BLK):
            at = g if kind == 0 else (g + BLK if g < BLK // 2 else g - BLK)
            for to in range(BLK):
                if at - to in cols:
                    kx = cols.index(at - to)
                    if name == "wca":
                        out[g, :, slot - n, to, :] = w[ky, kx, :, m * CH:(m + 1) * CH]
                    else:
                        out[g, :, slot - n, to, :] = w[ky, kx, m * CH:(m + 1) * CH, :]
    return out.reshape(P, -1, P)


def kernel(**inputs):
    import concourse.bacc as bacc
    from concourse.bass_utils import run_bass_kernel_spmd

    nc = bacc.Bacc("TRN2", target_bir_lowering=False, num_devices=1)
    a = {k.replace("L0_conv_", ""): np.ascontiguousarray(v) for k, v in inputs.items()}
    weights = np.concatenate([block_matrices(a[n], n) for n in CONVS], axis=1)
    bca = a["bca"].reshape(3, CH)
    a.update(bca0=bca[0], bca1=bca[1], bca2=bca[2])
    params = np.stack([np.tile(a[n], BLK) for n in COL], axis=1)
    code = a["L1_conv_codebook"]
    f32 = np.float32
    part = np.arange(P) % 32
    arrays = {
        "x": a["x"],
        "weights": weights,
        "params": np.ascontiguousarray(params),
        "codes4": np.ascontiguousarray(np.tile(code.T, (BLK, 1))),
        "codebook": code,
        "ident": np.eye(P, dtype=f32),
        "group_mean": np.tile(np.eye(CH, dtype=f32), (BLK, BLK)) / f32(BLK),
        "part_mask": np.stack([-(part > 0).astype(f32), -(part > 1).astype(f32)] * 2, axis=1),
    }
    names = ["x", "weights", "params", "codes4", "codebook", "ident", "group_mean", "part_mask"]
    args = [nc.dram_tensor(f"in_{n}", arrays[n].shape, F32, kind="ExternalInput").ap() for n in names]
    out = nc.dram_tensor("out", (IMAGES, HEIGHT, WIDTH, CH), F32, kind="ExternalOutput").ap()
    conv_vq_kernel(nc, *args, out)
    r = run_bass_kernel_spmd(nc, [{f"in_{n}": arrays[n] for n in names}], core_ids=[0])
    return r.results[0]["out"]
```

```python
import numpy as np
import concourse.bass as bass
from concourse import mybir
from concourse.alu_op_type import AluOpType as ALU
from contextlib import ExitStack

ACT = mybir.ActivationFunctionType
F32 = mybir.dt.float32
F32R = mybir.dt.float32r
U32 = mybir.dt.uint32

P = 128
IMAGES, HEIGHT, WIDTH, CH = 8, 128, 128, 32
CODES = 512
ROWS = HEIGHT // 2
COLS = WIDTH // 2
BLK = 4
JN = COLS // BLK
PAD = 2
RP = ROWS + 2 * PAD
HALF = JN // 2
MAP = JN * ROWS
XCHUNKS = 8
CW = WIDTH // XCHUNKS * CH
TILES = WIDTH
JTILES = TILES // JN
CTILES = TILES // XCHUNKS
BANKS = 4
PARTS = 3
STACKED = 16 * PARTS * BLK
KST = PARTS * CH + 2
LEAK = 0.3
PRIMED = 1
GN_EPS, BN_EPS = 1e-5, 1e-3
LL, HL, LH, HH = range(4)
BANDS = (LH, HL, HH)

CONVS = {
    "w15": (3, (-2, -1, 0, 1, 2), (-2, -1, 0, 1, 2)),
    "w13": (3, (-1, 0, 1), (-1, 0, 1)),
    "w25": (1, (-2, -1, 0, 1, 2), (-2, -1, 0, 1, 2)),
    "w12": (3, (0, 1), (0, 1)),
    "w23": (1, (-1, 0, 1), (-1, 0, 1)),
    "w22": (1, (0, 1), (0, 1)),
    "wd1": (1, (-2, 0, 2), (-2, 0, 2)),
    "wd2": (1, (-2, 0, 2), (-2, 0, 2)),
    "wd3": (1, (-2, 0, 2), (-2, 0, 2)),
    "wca": (3, (0,), (0,)),
    "wcb": (4, (-1, 0, 1), (-1, 0, 1)),
    "whf": (3, (0,), (0,)),
}
ONE_BY_ONE = ("wca", "whf")


def weight_slots():
    slots, first = {}, {}
    for name, (maps, rows, _) in CONVS.items():
        first[name] = len(slots)
        for m in range(maps):
            for kind in range(1 if name in ONE_BY_ONE else 2):
                for ky in range(len(rows)):
                    slots[name, m, kind, ky] = len(slots)
    first["end"] = len(slots)
    return slots, first


SLOTS, FIRST = weight_slots()
NW = FIRST["end"]

ORDER = ["w15", "w13", "w25", "w12", "w23", "w22", "wd1", "wd2", "wd3"]
GROUP = {}
for _n in ORDER:
    for _h in range(2):
        GROUP[_n, _h] = len(GROUP)
for _m in range(3):
    for _h in range(2):
        GROUP["wca", _m, _h] = len(GROUP)
for _n in ("whf", "wcb"):
    for _h in range(2):
        GROUP[_n, _h] = len(GROUP)
NG = len(GROUP)
RING = 4
assert NG % RING == 0

COL = {n: i for i, n in enumerate(["b15", "b13", "b12", "b25", "b23", "b22", "bd1", "bd2", "bd3", "bca0", "bca1",
                                   "bca2", "bcb", "bn_gamma", "bn_beta", "bn_mean", "bn_var", "bhf"])}


def make_plan():
    plan = []
    for n in ORDER:
        maps, rows, _ = CONVS[n]
        for kind in range(2):
            for half in range(2):
                for m in range(maps):
                    for ky in range(len(rows)):
                        plan.append(("mm", n, half, m, kind, ky))
    for m in range(3):
        for half in range(2):
            plan.append(("mm", "wca", half, m, 0, 0))
    lead = 34
    at = {lead: [("mean2",)], lead + 4: [("var2",)], lead + 8: [("bias2",)]}
    steps = [x for c in range(XCHUNKS)
             for x in [("ychunk", c)] + [("tile", t) for t in range(c * CTILES, (c + 1) * CTILES)]]
    places = [i for i in range(lead + 12, len(plan) - 6)
              if not (plan[i][1] in ("w22", "wd1", "wd2", "wd3") and plan[i][4] == 1)]
    for k, x in enumerate(steps):
        at.setdefault(places[k * len(places) // len(steps)], []).append(x)
    out = []
    for i, x in enumerate(plan):
        out += at.get(i, [])
        out.append(x)
    cb = []
    for m in range(4):
        if m == 3:
            cb += [("mm", "whf", half, 2, 0, 0) for half in range(2)]
        for kind in range(2):
            for half in range(2):
                for ky in range(3):
                    cb.append(("mm", "wcb", half, m, kind, ky))
        if m in (1, 2):
            cb += [("mm", "whf", half, m - 1, 0, 0) for half in range(2)]
        cb.append(("cbmap", m))
    for i, x in enumerate(cb):
        if i % 2 == 0 and i // 2 < XCHUNKS:
            out.append(("xchunk", i // 2))
        if i == 26:
            out.append(("mean1",))
        if i == 30:
            out.append(("var1",))
        out.append(x)
    return out


PLAN = make_plan()
MAKER = {"w25": "w15", "w23": "w13", "w22": "w12", "wd2": "wd1", "wd3": "wd2", "wca": "wd3"}
LEAKY = ORDER
HAS_EDGE = ["w15", "w13", "w12", "wd1", "wd2"]


def last_products():
    seen = {}
    for i, x in enumerate(PLAN):
        if x[0] == "mm":
            key = ("wca", x[3], x[2]) if x[1] == "wca" else (x[1], x[2])
            seen.setdefault(key, []).append(i)
    return {k: (v[0], v[-1]) for k, v in seen.items()}


SPAN = last_products()
MAP_DONE = [max(j for j in range(i) if PLAN[j][0] == "mm") for i, x in enumerate(PLAN) if x[0] == "cbmap"][:3]


EDGES = ((slice(0, P // 2), slice(1, JN), slice(0, JN - 1)),
         (slice(P // 2, P), slice(0, JN - 1), slice(1, JN)))


def wait(eng, sem, value):
    if not isinstance(value, int) or value > 0:
        eng.wait_ge(sem, value)


def wait_apart(eng, sem, value, passed):
    wait(eng, sem, value)
    eng.sem_inc(passed, 1)


def unit(c, t=None):
    return (CTILES + 1) * c + (0 if t is None else 1 + t)


def conv_vq_kernel(nc, x, weights, params, codes4, codebook, ident, group_mean, part_mask, out):
    ctx = ExitStack()
    with ctx:
        def sb(name, shape, dt=F32):
            return ctx.enter_context(nc.sbuf_tensor(name, shape, dt))

        def sem(name):
            return ctx.enter_context(nc.semaphore(name))

        w_sb = sb("w_sb", [P, NW, P])
        prm = sb("prm", [P, len(COL)])
        idn = sb("idn", [P, P])
        gmean = sb("gmean", [P, P])
        pmask = sb("pmask", [P, 4])
        cb4 = sb("cb4", [P, CODES])
        cbs = sb("cbs", [P, CODES])
        factors = sb("factors", [P, P])
        cst = sb("cst", [P, CODES], F32R)
        yh = sb("yh", [P, 2, 2, P], F32R)
        yl = sb("yl", [P, 2, 2, P], F32R)
        yst = sb("yst", [P, 2, BLK, 2, P], F32R)
        xnat = sb("xnat", [P, 2, CW])
        xord = sb("xord", [P, 2, CW])
        xt = sb("xt", [P, 2, 2, 2, 2, ROWS])
        sd = sb("sd", [P, 2, 2, 2, ROWS])
        chigh = xt[:, 0].rearrange("p w j e i -> p (w j e i)").bitcast(F32R)
        brest = sd[:, :].rearrange("p s j e i -> p (s j e i)")
        bands = [sb(f"bands{i}", [P, 2, JN, 2, ROWS]) for i in range(2)]
        hf = [[sb(f"hf{m}{k}", [P, JN, RP]) for k in range(2)] for m in range(3)]
        lln = [sb(f"lln{k}", [P, JN, RP]) for k in range(2)]
        ha = [sb(f"ha{k}", [P, JN, RP]) for k in range(2)]
        hb = [sb(f"hb{k}", [P, JN, RP]) for k in range(2)]
        br = [sb(f"br{m}", [P, JN, ROWS]) for m in range(3)]
        z = sb("z", [P, 2, HALF, ROWS])
        wtmp = z[:, :].rearrange("p e (j s) i -> p e j s i", s=2)
        ync = sb("ync", [P, 2, CW])
        vqc = sb("vqc", [P, 2, CW])
        idx = sb("idx", [P, 2, 16, 8], U32)
        top8 = sb("top8", [P, 4, 8])
        st1 = sb("st1", [P, XCHUNKS, 6])
        st2 = sb("st2", [P, XCHUNKS, 6])
        mv = [sb(f"mv{i}", [P, 2]) for i in range(2)]
        mall = [sb(f"mall{i}", [P, 1]) for i in range(2)]
        dev = [sb(f"dev{i}", [P, 1]) for i in range(2)]
        vsum = [sb(f"vsum{i}", [P, 1]) for i in range(2)]
        veps = [sb(f"veps{i}", [P, 1]) for i in range(2)]
        rstd = [sb(f"rstd{i}", [P, 1]) for i in range(2)]
        scale1 = sb("scale1", [P, 1])
        shift1 = sb("shift1", [P, 1])
        resid = [sb(f"resid{i}", [P, 1]) for i in range(2)]
        scale2 = sb("scale2", [P, 1])
        power = sb("power", [P, 1])
        bnv = sb("bnv", [P, 1])
        bnr = sb("bnr", [P, 1])
        bns = sb("bns", [P, 1])
        bnt = sb("bnt", [P, 1])
        bnb = sb("bnb", [P, 1])
        bnsh = sb("bnsh", [P, 1])
        bnbh = sb("bnbh", [P, 1])
        bhfh = sb("bhfh", [P, 1])

        ring = [ctx.enter_context(nc.psum_tensor(f"ring{i}", [P, HALF, ROWS], F32)) for i in range(RING)]
        score = [ctx.enter_context(nc.psum_tensor(f"score{i}", [P, CODES], F32)) for i in range(4)]

        s_w = {n: sem(f"s_w_{n}") for n in CONVS}
        s_const = sem("s_const")
        s_zero = sem("s_zero")
        s_init = sem("s_init")
        s_x = [sem(f"s_x{i}") for i in range(2)]
        s_xT = sem("s_xT")
        s_xord = sem("s_xord")
        s_xev = sem("s_xev")
        s_dwt = sem("s_dwt")
        s_agg = [sem(f"s_agg{i}") for i in range(2)]
        s_mean = [sem(f"s_mean{i}") for i in range(2)]
        s_dev = [sem(f"s_dev{i}") for i in range(2)]
        s_var = [sem(f"s_var{i}") for i in range(2)]
        s_veps = [sem(f"s_veps{i}") for i in range(2)]
        s_rstd = [sem(f"s_rstd{i}") for i in range(2)]
        s_norm = sem("s_norm")
        s_lln = sem("s_lln")
        s_hfw = sem("s_hfw")
        s_grp = sem("s_grp")
        s_free = sem("s_free")
        s_leaky = sem("s_leaky")
        s_edge = sem("s_edge")
        s_sum = sem("s_sum")
        s_phf = sem("s_phf")
        s_pedge = sem("s_pedge")
        s_cbmap = sem("s_cbmap")
        s_band = sem("s_band")
        s_neg = sem("s_neg")
        s_cbs = sem("s_cbs")
        s_bias = sem("s_bias")
        s_parts = sem("s_parts")
        s_yh = sem("s_yh")
        s_yl = sem("s_yl")
        s_yst = [sem(f"s_yst{i}") for i in range(2)]
        s_tile = sem("s_tile")
        s_idx = sem("s_idx")
        s_yT = sem("s_yT")
        s_yev = sem("s_yev")
        s_gather = [sem(f"s_gather{i}") for i in range(2)]
        s_add = sem("s_add")
        s_store = [sem(f"s_store{i}") for i in range(2)]
        s_yedge = sem("s_yedge")
        s_bnv = sem("s_bnv")
        s_bnr = sem("s_bnr")
        s_bn = sem("s_bn")
        s_passed = [sem(f"s_passed{i}") for i in range(3)]
        s_top = sem("s_top")
        s_d0, s_dn, s_dc, s_dq = (sem(n) for n in ("s_d0", "s_dn", "s_dc", "s_dq"))

        LEAKY_TILE = {"w15": ha, "w13": hb, "w12": ha, "wd1": ha, "wd2": hb, "wd3": ha}

        block = ctx.enter_context(nc.Block())
        xv = x.rearrange("b (i e) w c -> b e i (w c)", e=2)
        ov = out.rearrange("b (i e) w c -> b e i (w c)", e=2)

        def rounds(eng, body):
            body(0, 0, True, False, True)
            with eng.Fori(0, (IMAGES - 2) // 2) as i:
                body(2 * i + 1, 1, True, True, True)
                body(2 * i + 2, 0, True, True, True)
            body(IMAGES - 1, 1, True, True, False)
            body(IMAGES, 0, False, True, False)

        def own(tile, half, rows=slice(PAD, PAD + ROWS)):
            return tile[:, half * HALF:(half + 1) * HALF, rows]

        def raw(par, slot):
            return bands[par][:, slot // 2, :, slot % 2, :]

        @block.sync
        def _(sp):
            def load(b, k):
                wait(sp, s_xord, XCHUNKS * b + k - 1)
                for e in range(2):
                    sp.dma_start(xnat[e * ROWS:(e + 1) * ROWS, k % 2, :],
                                 xv[b, e, :, k * CW:(k + 1) * CW] if isinstance(b, int) else
                                 xv[bass.ds(b, 1), e, :, k * CW:(k + 1) * CW].rearrange("b i n -> (b i) n")
                                 ).then_inc(s_x[k % 2], 16)

            def store(v, c):
                sp.wait_ge(s_add, PRIMED + XCHUNKS * v + c + 1)
                for e in range(2):
                    sp.dma_start(ov[v, e, :, c * CW:(c + 1) * CW] if isinstance(v, int) else
                                 ov[bass.ds(v, 1), e, :, c * CW:(c + 1) * CW].rearrange("b i n -> (b i) n"),
                                 vqc[e * ROWS:(e + 1) * ROWS, c % 2, :]).then_inc(s_store[c % 2], 16)

            for dst, src in ((idn, ident), (gmean, group_mean), (prm, params), (cb4, codes4), (pmask, part_mask)):
                sp.dma_start(dst[:, :], src[:, :]).then_inc(s_const, 16)
            for k in range(XCHUNKS):
                load(0, k)

            def stack(v, j):
                if j >= 2:
                    wait_apart(sp, s_tile, TILES * v + JTILES * (j - 1), s_passed[2])
                sp.wait_ge(s_yl, JN * v + j + 1)
                for k, part in enumerate((yh, yl, yh)):
                    for g in range(BLK):
                        sp.dma_start(yst[k * CH:(k + 1) * CH, j % 2, g].bitcast(F32),
                                     part[g * CH:(g + 1) * CH, j % 2].bitcast(F32)).then_inc(s_yst[j % 2], 16)

            def body(b, par, conv, quant, nxt):
                if nxt:
                    for k in range(2):
                        load(b + 1, k)
                if quant:
                    for j in range(JN):
                        stack(b - 1, j)
                        if j >= 4 and j % 2 == 0:
                            store(b - 1, j // 2 - 2)
                    store(b - 1, XCHUNKS - 2)
                if nxt:
                    for k in range(2, XCHUNKS):
                        load(b + 1, k)
                if quant:
                    store(b - 1, XCHUNKS - 1)

            rounds(sp, body)
            for i in range(2):
                sp.wait_ge(s_store[i], PRIMED + 32 * (XCHUNKS // 2) * IMAGES)

        @block.tensor
        def _(pe):
            def transpose4(dst, src, last):
                for n in range(4):
                    t = nc.tensor.transpose(dst[:, n * P:(n + 1) * P], src(n), idn[:, :])
                t.then_inc(last, 1)

            def xchunk(b, k):
                pe.wait_ge(s_xord, XCHUNKS * b + k + 1)
                if k == 0:
                    wait(pe, s_veps[0], b)
                if k >= 4:
                    pe.wait_ge(s_xev, XCHUNKS * b + k - 3)
                else:
                    wait(pe, s_idx, TILES * (b - 1))
                transpose4(score[k % 4], lambda n: xord[:, k % 2, n * P:(n + 1) * P], s_xT)

            def combine(which, src, col, ready, n, done):
                pe.wait_ge(ready, n + 1)
                nc.tensor.matmul(score[col][:, 0:1], gmean[:, :], src, start=True, stop=True).then_inc(done, 1)

            def mean(which, n):
                if which == 0:
                    pe.wait_ge(s_xev, XCHUNKS * (n + 1))
                combine(which, mv[which][:, 0:1], 0, s_agg[which], n, s_mean[which])

            def var(which, n):
                combine(which, vsum[which][:, :], 1, s_dev[which], n, s_var[which])

            def bias2(v):
                pe.wait_ge(s_neg, v + 1)
                pe.wait_ge(s_cbs, v + 1)
                nc.tensor.matmul(score[2][:, :], factors[:, :], cbs[:, :], start=True, stop=True)\
                    .then_inc(s_bias, 1)

            def yview(par, wp, j):
                return bands[par][:, wp, j].rearrange("p e i -> p (e i)")

            def bank_free(v, u):
                if u < BANKS:
                    pe.wait_ge(s_parts, v + 1)
                    return
                c, t = divmod(u - BANKS, CTILES + 1)
                if t == 0:
                    pe.wait_ge(s_yev, XCHUNKS * v + c + 1)
                else:
                    pe.wait_ge(s_idx, TILES * v + CTILES * c + t)

            def ychunk(v, par, c):
                bank_free(v, unit(c))
                transpose4(score[unit(c) % BANKS], lambda n: yview(par, n % 2, 2 * c + n // 2), s_yT)

            def tile(v, t):
                c, j = t // CTILES, t // JTILES
                u = unit(c, t % CTILES)
                bank_free(v, u)
                if t % JTILES == 0:
                    pe.wait_ge(s_yst[j % 2], STACKED * ((JN // 2) * v + j // 2 + 1))
                wp, g = t % JTILES // BLK, t % BLK
                nc.tensor.matmul(score[u % BANKS][:, :], yst[0:KST, j % 2, g, wp], cst[0:KST, :],
                                 start=True, stop=True).then_inc(s_tile, 1)

            def sources(n, m):
                if n in ("w15", "w13", "w12"):
                    return hf[m]
                if n == "wcb":
                    return lln if m == 0 else hf[m - 1]
                if n == "whf":
                    return hf[m]
                return {"w25": ha, "w23": hb, "w22": ha, "wd1": hb, "wd2": ha, "wd3": hb, "wca": ha}[n]

            def inputs_ready(b, n, half, m, kind, new):
                if n == "w15" and half == 0:
                    pe.wait_ge(s_hfw, 6 * b + (m + 1 if kind == 0 else m + 4))
                elif n in MAKER and m == 0:
                    if kind == 0:
                        pe.wait_ge(s_leaky, len(LEAKY) * 2 * b + GROUP[MAKER[n], half] + 1)
                    elif half == 0:
                        pe.wait_ge(s_edge, len(HAS_EDGE) * b + HAS_EDGE.index(MAKER[n]) + 1)
                elif n == "wd1":
                    if kind == 0:
                        pe.wait_ge(s_sum, 2 * b + half + 1)
                    elif half == 0:
                        pe.wait_ge(s_yedge, b + 1)
                elif n == "wcb":
                    if m == 0:
                        if half == 0 and kind == 0:
                            pe.wait_ge(s_lln, b + 1)
                    elif kind == 0:
                        pe.wait_ge(s_phf, 6 * b + 2 * (m - 1) + half + 1)
                    elif half == 0:
                        pe.wait_ge(s_pedge, 3 * b + m)
                elif n == "whf" and m == 2:
                    pe.wait_ge(s_phf, 6 * b + 2 * m + half + 1)

            def product(i, b, n, half, m, kind, ky, seen):
                key = ("wca", m, half) if n == "wca" else (n, half)
                first, last = SPAN[key]
                g = GROUP[key]
                if i == first:
                    wait(pe, s_free, NG * b + g - (RING - 1))
                if (n, half, m, kind) not in seen:
                    seen.add((n, half, m, kind))
                    if isinstance(b, int) and b == 0 and ("w", n) not in seen:
                        seen.add(("w", n))
                        pe.wait_ge(s_w[n], 16)
                    inputs_ready(b, n, half, m, kind, seen)
                di = CONVS[n][1][ky]
                t = nc.tensor.matmul(ring[g % RING][:, :, :], w_sb[:, SLOTS[n, m, kind, ky], :],
                                     own(sources(n, m)[kind], half, slice(PAD + di, PAD + di + ROWS)),
                                     start=(i == first), stop=(i == last))
                if i == last:
                    t.then_inc(s_grp, 1)
                elif i in MAP_DONE:
                    t.then_inc(s_cbmap, 1)

            def body(b, par, conv, quant, nxt):
                seen, v = set(), b - 1
                for i, step in enumerate(PLAN):
                    what = step[0]
                    if what == "mm" and conv:
                        product(i, b, *step[1:], seen)
                    elif quant and what == "mean2":
                        mean(1, v)
                    elif quant and what == "var2":
                        var(1, v)
                    elif quant and what == "bias2":
                        bias2(v)
                    elif quant and what == "ychunk":
                        ychunk(v, 1 - par, step[1])
                    elif quant and what == "tile":
                        tile(v, step[1])
                    elif nxt and what == "xchunk":
                        xchunk(b + 1, step[1])
                    elif nxt and what == "mean1":
                        mean(0, b + 1)
                    elif nxt and what == "var1":
                        var(0, b + 1)

            pe.wait_ge(s_const, 16 * 5)
            pe.wait_ge(s_init, 1)
            for k in range(XCHUNKS):
                xchunk(0, k)
            mean(0, 0)
            var(0, 0)
            rounds(pe, body)

        @block.scalar
        def _(act):
            for n in CONVS:
                hi = min([f for f in FIRST.values() if f > FIRST[n]])
                act.dma_start(w_sb[:, FIRST[n]:hi, :], weights[:, FIRST[n]:hi, :]).then_inc(s_w[n], 16)

            def col(name):
                return prm[:, COL[name]:COL[name] + 1]

            def edge_copy(tiles):
                for p, src, dst in EDGES:
                    t = nc.scalar.copy(tiles[1][p, dst, PAD:PAD + ROWS], tiles[0][p, src, PAD:PAD + ROWS])
                return t

            def evacuate(b, key):
                g = GROUP[key]
                n, half = key[0], key[-1]
                bank = ring[g % RING]
                act.wait_ge(s_grp, NG * b + g + 1)
                if n in LEAKY:
                    wait(act, s_leaky, len(LEAKY) * 2 * b + g - 1)
                    nc.scalar.activation(z[:, g % 2], bank[:, :, :], ACT.Identity, bias=col("b" + n[1:]))\
                        .then_inc(s_free, 1)
                    if half == 1 and n in HAS_EDGE:
                        act.wait_ge(s_leaky, len(LEAKY) * 2 * b + g + 1)
                        edge_copy(LEAKY_TILE[n]).then_inc(s_edge, 1)
                    if half == 1 and n == "w22":
                        act.wait_ge(s_sum, 2 * b + 2)
                        edge_copy(hb).then_inc(s_yedge, 1)
                elif n == "wca":
                    m = key[1]
                    t = nc.scalar.activation(br[m][:, half * HALF:(half + 1) * HALF, :], bank[:, :, :],
                                             ACT.Sigmoid, bias=col(f"bca{m}"))
                    t.then_inc(s_free, 1)
                    if m == 2 and half == 1:
                        for k in range(3):
                            act.wait_ge(s_phf, 6 * b + 2 * k + 2)
                            edge_copy(hf[k]).then_inc(s_pedge, 1)
                elif n == "whf":
                    t = nc.scalar.activation(br[2][:, half * HALF:(half + 1) * HALF, :], bank[:, :, :],
                                             ACT.Identity, bias=bhfh[:, :], scale=0.5)
                    t.then_inc(s_free, 1)
                else:
                    nc.scalar.activation(br[0][:, half * HALF:(half + 1) * HALF, :], bank[:, :, :],
                                         ACT.Identity, bias=bnbh[:, :], scale=bnsh[:, :])
                    t = nc.scalar.activation(br[1][:, half * HALF:(half + 1) * HALF, :], bank[:, :, :],
                                             ACT.Sigmoid, bias=bnb[:, :], scale=bns[:, :])
                    t.then_inc(s_free, 1)

            def high(v, par, j):
                act.wait_ge(s_agg[1], v + 1)
                if j >= 2:
                    act.wait_ge(s_yst[j % 2], STACKED * ((JN // 2) * v + j // 2))
                nc.scalar.copy(yh[:, j % 2], bands[par][:, :, j].rearrange("p w e i -> p w (e i)"))\
                    .then_inc(s_yh, 1)

            def xorder(b, k):
                act.wait_ge(s_x[k % 2], 32 * ((XCHUNKS // 2) * b + k // 2 + 1))
                wait(act, s_xT, XCHUNKS * b + k - 1)
                src = xnat[:, k % 2, :].rearrange("p (j g w c) -> p w j g c", g=4, w=2, c=CH)
                dst = xord[:, k % 2, :].rearrange("p (w j g c) -> p w j g c", w=2, g=4, c=CH)
                for w in range(2):
                    t = nc.scalar.copy(dst[:, w], src[:, w])
                t.then_inc(s_xord, 1)

            def xcopy(b, k):
                if k + 2 < XCHUNKS:
                    xorder(b, k + 2)
                act.wait_ge(s_xT, XCHUNKS * b + k + 1)
                wait(act, s_dwt, XCHUNKS * b + k - 1)
                nc.scalar.copy(xt[:, k % 2].rearrange("p w j e i -> p (w j e i)"), score[k % 4][:, :])\
                    .then_inc(s_xev, 1)

            def ycopy(v, c):
                act.wait_ge(s_yT, XCHUNKS * v + c + 1)
                act.wait_ge(s_add, PRIMED + XCHUNKS * v + max(c - 1, 0))
                dst = ync[:, c % 2, :].rearrange("p (j g w c) -> p j w g c", g=4, w=2, c=CH)
                src = score[unit(c) % BANKS][:, :].rearrange("p (j w g c) -> p j w g c", g=4, w=2, c=CH)
                for j in range(2):
                    t = nc.scalar.copy(dst[:, j], src[:, j])
                t.then_inc(s_yev, 1)

            def normal_ll(n, par):
                act.wait_ge(s_norm, n + 1)
                wait(act, s_cbmap, 3 * (n - 1) + 1)
                src = raw(par, LL)
                nc.scalar.activation(lln[0][:, :, PAD:PAD + ROWS], src, ACT.Identity, bias=shift1[:, :],
                                     scale=scale1[:, :])
                for p, s, d in EDGES:
                    t = nc.scalar.activation(lln[1][p, d, PAD:PAD + ROWS], src[p, s], ACT.Identity,
                                             bias=shift1[p, :], scale=scale1[p, :])
                t.then_inc(s_lln, 1)

            def normal_own(n, par, m):
                if m < 2:
                    wait(act, s_cbmap, 3 * (n - 1) + m + 2)
                else:
                    wait(act, s_grp, NG * n)
                nc.scalar.activation(hf[m][0][:, :, PAD:PAD + ROWS], raw(par, BANDS[m]), ACT.Identity,
                                     bias=0.0, scale=scale1[:, :]).then_inc(s_hfw, 1)

            def normal_edge(n, par, m):
                for p, s, d in EDGES:
                    t = nc.scalar.activation(hf[m][1][p, d, PAD:PAD + ROWS], raw(par, BANDS[m])[p, s],
                                             ACT.Identity, bias=0.0, scale=scale1[p, :])
                t.then_inc(s_hfw, 1)

            def body(b, par, conv, quant, nxt):
                v = b - 1
                for i, step in enumerate(PLAN):
                    what = step[0]
                    if nxt and i == 0:
                        for k in range(2):
                            xorder(b + 1, k)
                    if quant and what == "mean2":
                        for j in range(2):
                            high(v, 1 - par, j)
                    elif quant and what == "tile":
                        if step[1] % JTILES == JTILES // 2 and step[1] // JTILES + 2 < JN:
                            high(v, 1 - par, step[1] // JTILES + 2)
                    elif quant and what == "ychunk":
                        ycopy(v, step[1])
                    elif nxt and what == "xchunk":
                        xcopy(b + 1, step[1])
                    elif nxt and what == "cbmap" and step[1] == 2:
                        normal_ll(b + 1, 1 - par)
                        normal_own(b + 1, 1 - par, 0)
                        normal_own(b + 1, 1 - par, 1)
                    elif conv and what == "mm":
                        for key, (_, last) in SPAN.items():
                            if last == i:
                                evacuate(b, key)
                if nxt:
                    normal_own(b + 1, 1 - par, 2)
                    for m in range(3):
                        normal_edge(b + 1, 1 - par, m)

            act.wait_ge(s_zero, 1)
            act.wait_ge(s_bn, 1)
            for k in range(2):
                xorder(0, k)
            for k in range(XCHUNKS):
                xcopy(0, k)
            normal_ll(0, 0)
            for m in range(3):
                normal_own(0, 0, m)
            for m in range(3):
                normal_edge(0, 0, m)
            rounds(act, body)

        @block.vector
        def _(dve):
            def after(ins, sem, value):
                ins.then_inc(sem, 1)
                dve.wait_ge(sem, value)

            def statistics(which, n, sem, base):
                dve.wait_ge(s_mean[which], n + 1)
                after(nc.vector.tensor_copy(mall[which][:, :], score[0][:, 0:1]), sem, base + 1)
                after(nc.vector.tensor_tensor(dev[which][:, :], mv[which][:, 0:1], mall[which][:, :],
                                              ALU.subtract), sem, base + 2)
                nc.vector.scalar_tensor_tensor(out=vsum[which][:, :], in0=dev[which][:, :],
                                               scalar=dev[which][:, :], in1=mv[which][:, 1:2], op0=ALU.mult,
                                               op1=ALU.add).then_inc(s_dev[which], 1)

            def variance(which, n):
                dve.wait_ge(s_var[which], n + 1)
                nc.vector.tensor_scalar_add(veps[which][:, :], score[1][:, 0:1], GN_EPS).then_inc(s_veps[which], 1)
                dve.wait_ge(s_rstd[which], n + 1)

            NSTEP = 2 * XCHUNKS + 4

            def xchunk(n, par, k):
                base = NSTEP * n + 2 * k
                dve.wait_ge(s_xev, XCHUNKS * n + k + 1)
                slot = xt[:, k % 2]
                nc.vector.bn_stats(st1[:, k, :], slot.rearrange("p w j e i -> p (w j e i)"))
                wait(dve, s_dwt, XCHUNKS * n + k)
                nc.vector.tensor_tensor(sd[:, 0], slot[:, 0], slot[:, 1], ALU.add).then_inc(s_dn, 1)
                nc.vector.tensor_tensor(sd[:, 1], slot[:, 1], slot[:, 0], ALU.subtract).then_inc(s_dn, 1)
                dve.wait_ge(s_dn, base + 2)
                js = slice(2 * k, 2 * k + 2)
                pair = sd[:, :].rearrange("p s j e i -> p e j s i")
                nc.vector.tensor_tensor(bands[par][:, 0, js], pair[:, 0], pair[:, 1], ALU.add)
                nc.vector.tensor_tensor(bands[par][:, 1, js], pair[:, 1], pair[:, 0], ALU.subtract)\
                    .then_inc(s_dwt, 1)

            def aggregate1(n):
                wait_apart(dve, s_dwt, XCHUNKS * (n + 1), s_passed[0])
                nc.vector.bn_aggr(mv[0][:, :], st1[:, :, :]).then_inc(s_agg[0], 1)

            def mean1(n):
                statistics(0, n, s_dn, NSTEP * n + 2 * XCHUNKS)

            def var1(n, par):
                variance(0, n)
                wait(dve, s_hfw, 6 * n)
                nc.vector.tensor_scalar_mul(scale1[:, :], rstd[0][:, :], 0.5).then_inc(s_dn, 1)
                nc.vector.tensor_scalar(resid[par][:, :], rstd[0][:, :], 0.25, 0.25, ALU.mult, ALU.add)\
                    .then_inc(s_dn, 1)
                dve.wait_ge(s_dn, NSTEP * (n + 1))
                nc.vector.tensor_scalar(shift1[:, :], mall[0][:, :], rstd[0][:, :], -2.0, ALU.mult, ALU.mult)\
                    .then_inc(s_norm, 1)

            def leaky(b, n, half):
                g = GROUP[n, half]
                js = slice(half * HALF, (half + 1) * HALF)
                dst = own(LEAKY_TILE[n][0], half) if n in LEAKY_TILE else br[("w25", "w23", "w22").index(n)][:, js, :]
                dve.wait_ge(s_free, NG * b + g + 1)
                nc.vector.scalar_tensor_tensor(out=dst, in0=z[:, g % 2], scalar=LEAK, in1=z[:, g % 2],
                                               op0=ALU.mult, op1=ALU.max).then_inc(s_leaky, 1)

            def branch_sum(b, half):
                js = slice(half * HALF, (half + 1) * HALF)
                dve.wait_ge(s_leaky, len(LEAKY) * 2 * b + GROUP["w22", half] + 1)
                after(nc.vector.tensor_tensor(br[0][:, js, :], br[0][:, js, :], br[1][:, js, :], ALU.add),
                      s_dc, 2 * b + half + 1)
                nc.vector.tensor_tensor(own(hb[0], half), br[0][:, js, :], br[2][:, js, :], ALU.add)\
                    .then_inc(s_sum, 1)

            QSTEP = 1 + 2 + 4 * 4 + 1 + 2 + 1 + 3

            def finish(v, par):
                bn = bands[par]
                part = wtmp[:, :].rearrange("p e j s i -> p s j e i")
                base = QSTEP * v
                dve.wait_ge(s_free, NG * (v + 1))
                after(nc.vector.tensor_tensor(br[0][:, :, :], br[0][:, :, :], br[1][:, :, :], ALU.mult),
                      s_dq, base + 1)
                dve.wait_ge(s_hfw, 6 * v + 6)
                nc.vector.scalar_tensor_tensor(out=raw(par, LL), in0=raw(par, LL), scalar=0.25, in1=br[0][:, :, :],
                                               op0=ALU.mult, op1=ALU.add).then_inc(s_dq, 1)
                nc.vector.tensor_scalar(bn[:, :, :, 1], bn[:, :, :, 1], resid[par][:, :], None, ALU.mult)\
                    .then_inc(s_dq, 1)
                nc.vector.scalar_tensor_tensor(out=raw(par, LH), in0=raw(par, LH), scalar=0.25, in1=br[2][:, :, :],
                                               op0=ALU.mult, op1=ALU.add).then_inc(s_band, 1)
                dve.wait_ge(s_dq, base + 3)
                dve.wait_ge(s_band, v + 1)
                for r in range(4):
                    js = slice(r * JN // 4, (r + 1) * JN // 4)
                    at = base + 4 + 4 * r
                    nc.vector.tensor_tensor(wtmp[:, 0], bn[:, 0, js], bn[:, 1, js], ALU.subtract)\
                        .then_inc(s_dq, 1)
                    nc.vector.tensor_tensor(wtmp[:, 1], bn[:, 0, js], bn[:, 1, js], ALU.add)\
                        .then_inc(s_dq, 1)
                    dve.wait_ge(s_dq, at + 1)
                    nc.vector.tensor_tensor(bn[:, 0, js], part[:, 0], part[:, 1], ALU.subtract)\
                        .then_inc(s_dq, 1)
                    nc.vector.tensor_tensor(bn[:, 1, js], part[:, 0], part[:, 1], ALU.add)\
                        .then_inc(s_dq, 1)
                    dve.wait_ge(s_dq, at + 3)
                flat = bn[:, :].rearrange("p w j e i -> p (w j e i)")
                for k in range(8):
                    t = nc.vector.bn_stats(st2[:, k, :], flat[:, k * 512:(k + 1) * 512])
                t.then_inc(s_dq, 1)
                wait_apart(dve, s_dq, base + 20, s_passed[0])
                nc.vector.bn_aggr(mv[1][:, :], st2[:, :, :]).then_inc(s_agg[1], 1)

            def var2(v):
                variance(1, v)
                base = QSTEP * v + 22
                after(nc.vector.tensor_scalar_mul(scale2[:, :], rstd[1][:, :], 2.0), s_dq, base + 1)
                nc.vector.tensor_scalar(factors[0:CH, :], idn[0:CH, :], 0.0, mall[1][0:CH, :],
                                        ALU.mult, ALU.subtract).then_inc(s_neg, 1)
                nc.vector.tensor_scalar(cbs[0:3 * CH, :], cb4[0:3 * CH, :], scale2[0:3 * CH, :], None, ALU.mult)\
                    .then_inc(s_cbs, 1)

            def bias2(v):
                base = QSTEP * v + 23
                hh, lo, bb = slice(0, 2 * CH), slice(2 * CH, 3 * CH), slice(3 * CH, KST)
                dve.wait_ge(s_cbs, v + 1)
                nc.vector.tensor_copy(cst[hh, :], cbs[hh, :])
                after(nc.vector.tensor_copy(chigh[lo, :], cbs[lo, :]), s_dq, base + 1)
                nc.vector.tensor_tensor(cst[lo, :], cbs[lo, :], chigh[lo, :], ALU.subtract)
                dve.wait_ge(s_bias, v + 1)
                after(nc.vector.tensor_copy(chigh[bb, :], score[2][bb, :]), s_dq, base + 2)
                after(nc.vector.scalar_tensor_tensor(out=brest[bb, :], in0=chigh[bb, :], scalar=pmask[bb, 0:1],
                                                     in1=score[2][bb, :], op0=ALU.mult, op1=ALU.add),
                      s_dq, base + 3)
                nc.vector.tensor_copy(cst[bb, :], brest[bb, :]).then_inc(s_parts, 1)

            def maximum(v, t):
                u = unit(t // CTILES, t % CTILES)
                if t % CTILES == 0:
                    c = t // CTILES
                    dve.wait_ge(s_add, PRIMED + XCHUNKS * v + max(c - 1, 0))
                wait_apart(dve, s_tile, TILES * v + t + 1, s_passed[0])
                nc.vector.max(top8[:, t % 4, :], score[u % BANKS][:, :]).then_inc(s_top, 1)

            def index(v, t):
                u = unit(t // CTILES, t % CTILES)
                wait_apart(dve, s_top, TILES * v + t + 1, s_passed[0])
                nc.vector.max_index(idx[:, t // CTILES % 2, t % CTILES, :], top8[:, t % 4, :],
                                    score[u % BANKS][:, :]).then_inc(s_idx, 1)

            def body(b, par, conv, quant, nxt):
                v = b - 1
                if quant:
                    finish(v, 1 - par)
                for i, step in enumerate(PLAN):
                    what = step[0]
                    if quant and what == "mean2":
                        statistics(1, v, s_dq, QSTEP * v + 20)
                    elif quant and what == "var2":
                        var2(v)
                    elif quant and what == "bias2":
                        bias2(v)
                    elif quant and what == "tile":
                        t = step[1]
                        maximum(v, t)
                        if t:
                            index(v, t - 1)
                        if t == TILES - 1:
                            index(v, t)
                    elif nxt and what == "xchunk":
                        xchunk(b + 1, 1 - par, step[1])
                        if step[1] == XCHUNKS - 1:
                            aggregate1(b + 1)
                    elif nxt and what == "mean1":
                        mean1(b + 1)
                    elif nxt and what == "var1":
                        var1(b + 1, 1 - par)
                    elif conv and what == "mm":
                        n, half = step[1], step[2]
                        if n in LEAKY and SPAN[n, half][1] == i:
                            leaky(b, n, half)
                            if n == "w22":
                                branch_sum(b, half)

            squares = slice(3 * CH, P)
            nc.vector.memset(factors[0:3 * CH, :], 0.0)
            nc.vector.memset(yst[3 * CH:KST].bitcast(F32).rearrange("p s g w n -> p (s g w n)"), 1.0)
            nc.vector.memset(factors[squares, :], -1.0).then_inc(s_init, 1)
            dve.wait_ge(s_const, 16 * 5)
            after(nc.vector.tensor_tensor(cbs[squares, :], cb4[squares, :], cb4[squares, :], ALU.mult), s_d0, 1)

            def col(name):
                return prm[:, COL[name]:COL[name] + 1]

            nc.vector.tensor_scalar_add(bnv[:, :], col("bn_var"), BN_EPS).then_inc(s_bnv, 1)
            dve.wait_ge(s_bnr, 1)
            after(nc.vector.tensor_tensor(bns[:, :], bnr[:, :], col("bn_gamma"), ALU.mult), s_d0, 2)
            after(nc.vector.tensor_tensor(bnt[:, :], col("bcb"), col("bn_mean"), ALU.subtract), s_d0, 3)
            after(nc.vector.scalar_tensor_tensor(out=bnb[:, :], in0=bnt[:, :], scalar=bns[:, :],
                                                 in1=col("bn_beta"), op0=ALU.mult, op1=ALU.add), s_d0, 4)
            nc.vector.tensor_scalar_mul(bnsh[:, :], bns[:, :], 0.5)
            nc.vector.tensor_scalar_mul(bnbh[:, :], bnb[:, :], 0.5)
            nc.vector.tensor_scalar_mul(bhfh[:, :], col("bhf"), 0.5).then_inc(s_bn, 1)
            for k in range(XCHUNKS):
                xchunk(0, 0, k)
            aggregate1(0)
            mean1(0)
            var1(0, 0)
            rounds(dve, body)

        @block.gpsimd
        def _(pool):
            def rsqrt(dst, src, done):
                nc.gpsimd.tensor_tensor(dst[:, :], src[:, :], power[:, :], ALU.pow).then_inc(done, 1)

            def norm(which, n):
                pool.wait_ge(s_veps[which], n + 1)
                rsqrt(rstd[which], veps[which], s_rstd[which])

            def gather(v, t):
                c, k = t // CTILES, t % CTILES
                if k == 0:
                    pool.wait_ge(s_store[c % 2], PRIMED + 32 * ((XCHUNKS // 2) * v + c // 2))
                wait_apart(pool, s_idx, TILES * v + t + 1, s_passed[1])
                w = 8 * (k // JTILES) + 2 * (k % BLK) + k % JTILES // BLK
                nc.gpsimd.indirect_dma_start(
                    vqc[:, c % 2, w * CH:(w + 1) * CH], None, codebook[:, :],
                    bass.IndirectOffsetOnAxis(idx[:, c % 2, k, 0:1], 0)).then_inc(s_gather[c % 2], 16)

            def low(v, par, j):
                pool.wait_ge(s_yh, JN * v + j + 1)
                nc.gpsimd.tensor_tensor(yl[:, j % 2], bands[par][:, :, j].rearrange("p w e i -> p w (e i)"),
                                        yh[:, j % 2], ALU.subtract).then_inc(s_yl, 1)

            def add(v, c):
                pool.wait_ge(s_yev, XCHUNKS * v + c + 1)
                pool.wait_ge(s_gather[c % 2], 256 * ((XCHUNKS // 2) * v + c // 2 + 1))
                nc.gpsimd.tensor_tensor(vqc[:, c % 2, :], vqc[:, c % 2, :], ync[:, c % 2, :], ALU.add)\
                    .then_inc(s_add, 1)

            def attend(b, m):
                for half in range(2):
                    js = slice(half * HALF, (half + 1) * HALF)
                    pool.wait_ge(s_free, NG * b + GROUP["wca", m, half] + 1)
                    nc.gpsimd.tensor_tensor(own(hf[m][0], half), own(hf[m][0], half), br[m][:, js, :], ALU.mult)\
                        .then_inc(s_phf, 1)

            def body(b, par, conv, quant, nxt):
                v = b - 1
                for i, step in enumerate(PLAN):
                    what = step[0]
                    if quant and what == "mean2":
                        for j in range(2):
                            low(v, 1 - par, j)
                    elif quant and what == "var2":
                        norm(1, v)
                    elif quant and what == "tile":
                        t = step[1]
                        if t % JTILES == JTILES // 2 and t // JTILES + 2 < JN:
                            low(v, 1 - par, t // JTILES + 2)
                        gather(v, t)
                        if t % CTILES == 5 and t > CTILES:
                            add(v, t // CTILES - 1)
                    elif nxt and what == "var1":
                        norm(0, b + 1)
                    elif conv and what == "mm":
                        for m in range(3):
                            if SPAN["wca", m, 1][1] == i:
                                attend(b, m)
                        if quant and SPAN["wca", 2, 1][1] == i:
                            add(v, XCHUNKS - 1)
                if quant and not conv:
                    add(v, XCHUNKS - 1)

            for counter in (s_add, *s_store):
                pool.sem_inc(counter, PRIMED)
            nc.gpsimd.memset(power[:, :], -0.5)
            tiles = [t for pair in (*hf, lln, ha, hb) for t in pair]
            for t in tiles:
                last = nc.gpsimd.memset(t[:, :, :], 0.0)
            last.then_inc(s_zero, 1)
            pool.wait_ge(s_zero, 1)
            pool.wait_ge(s_bnv, 1)
            rsqrt(bnr, bnv, s_bnr)
            norm(0, 0)
            rounds(pool, body)

    return nc



def block_matrices(w, name):
    maps, rows, cols = CONVS[name]
    n = FIRST[name]
    out = np.zeros((BLK, CH, len([k for k in SLOTS if k[0] == name]), BLK, CH), w.dtype)
    for (conv, m, kind, ky), slot in SLOTS.items():
        if conv != name:
            continue
        for g in range(BLK):
            at = g if kind == 0 else (g + BLK if g < BLK // 2 else g - BLK)
            for to in range(BLK):
                if at - to in cols:
                    kx = cols.index(at - to)
                    if name == "wca":
                        out[g, :, slot - n, to, :] = w[ky, kx, :, m * CH:(m + 1) * CH]
                    else:
                        out[g, :, slot - n, to, :] = w[ky, kx, m * CH:(m + 1) * CH, :]
    return out.reshape(P, -1, P)


def kernel(**inputs):
    import concourse.bacc as bacc
    from concourse.bass_utils import run_bass_kernel_spmd

    nc = bacc.Bacc("TRN2", target_bir_lowering=False, num_devices=1)
    a = {k.replace("L0_conv_", ""): np.ascontiguousarray(v) for k, v in inputs.items()}
    weights = np.concatenate([block_matrices(a[n], n) for n in CONVS], axis=1)
    bca = a["bca"].reshape(3, CH)
    a.update(bca0=bca[0], bca1=bca[1], bca2=bca[2])
    params = np.stack([np.tile(a[n], BLK) for n in COL], axis=1)
    code = a["L1_conv_codebook"]
    f32 = np.float32
    part = np.arange(P) % 32
    arrays = {
        "x": a["x"],
        "weights": weights,
        "params": np.ascontiguousarray(params),
        "codes4": np.ascontiguousarray(np.tile(code.T, (BLK, 1))),
        "codebook": code,
        "ident": np.eye(P, dtype=f32),
        "group_mean": np.tile(np.eye(CH, dtype=f32), (BLK, BLK)) / f32(BLK),
        "part_mask": np.stack([-(part > 0).astype(f32), -(part > 1).astype(f32)] * 2, axis=1),
    }
    names = ["x", "weights", "params", "codes4", "codebook", "ident", "group_mean", "part_mask"]
    args = [nc.dram_tensor(f"in_{n}", arrays[n].shape, F32, kind="ExternalInput").ap() for n in names]
    out = nc.dram_tensor("out", (IMAGES, HEIGHT, WIDTH, CH), F32, kind="ExternalOutput").ap()
    conv_vq_kernel(nc, *args, out)
    r = run_bass_kernel_spmd(nc, [{f"in_{n}": arrays[n] for n in names}], core_ids=[0])
    return r.results[0]["out"]
```

```python
import numpy as np
import concourse.bass as bass
from concourse import mybir
from concourse.alu_op_type import AluOpType as ALU
from contextlib import ExitStack

ACT = mybir.ActivationFunctionType
F32 = mybir.dt.float32
F32R = mybir.dt.float32r
U32 = mybir.dt.uint32

P = 128
IMAGES, HEIGHT, WIDTH, CH = 8, 128, 128, 32
CODES = 512
ROWS = HEIGHT // 2
COLS = WIDTH // 2
BLK = 4
JN = COLS // BLK
PAD = 2
RP = ROWS + 2 * PAD
HALF = JN // 2
MAP = JN * ROWS
XCHUNKS = 8
CW = WIDTH // XCHUNKS * CH
SIDE_LL = 3
TILES = WIDTH
JTILES = TILES // JN
CTILES = TILES // XCHUNKS
XTURN = 10
LEAD, REAR = 9, 13
BANKS = 4
PARTS = 3
STACKED = 16 * PARTS * BLK
KST = PARTS * CH + 2
LEAK = 0.3
PRIMED = 1
GN_EPS, BN_EPS = 1e-5, 1e-3
LL, HL, LH, HH = range(4)
BANDS = (LH, HL, HH)

CONVS = {
    "w15": (3, (-2, -1, 0, 1, 2), (-2, -1, 0, 1, 2)),
    "w13": (3, (-1, 0, 1), (-1, 0, 1)),
    "w25": (1, (-2, -1, 0, 1, 2), (-2, -1, 0, 1, 2)),
    "w12": (3, (0, 1), (0, 1)),
    "w23": (1, (-1, 0, 1), (-1, 0, 1)),
    "w22": (1, (0, 1), (0, 1)),
    "wd1": (1, (-2, 0, 2), (-2, 0, 2)),
    "wd2": (1, (-2, 0, 2), (-2, 0, 2)),
    "wd3": (1, (-2, 0, 2), (-2, 0, 2)),
    "wca": (3, (0,), (0,)),
    "wcb": (4, (-1, 0, 1), (-1, 0, 1)),
    "whf": (3, (0,), (0,)),
}
OWN, EDGE, LEFT, RIGHT = range(4)
KINDS = {"w15": (OWN, EDGE), "w13": (OWN, LEFT, RIGHT), "w25": (OWN, EDGE), "w12": (OWN, RIGHT),
         "w23": (OWN, EDGE), "w22": (OWN, EDGE), "wd1": (OWN, EDGE), "wd2": (OWN, EDGE), "wd3": (OWN, EDGE),
         "wca": (OWN,), "wcb": (OWN, LEFT, RIGHT), "whf": (OWN,)}
PACKED = {"w23": ((-1, False), (0, True)), "w22": ((0, True),)}


def row_offsets(name, kind):
    if kind == EDGE and name in PACKED:
        return [off for off, _ in PACKED[name]]
    return CONVS[name][1]


def maps_of(name, kind):
    return range(CONVS[name][0] if kind in (OWN, EDGE) else 1)


def weight_slots():
    slots, first = {}, {}
    for name in CONVS:
        first[name] = len(slots)
        for kind in KINDS[name]:
            for m in maps_of(name, kind):
                for ky in range(len(row_offsets(name, kind))):
                    slots[name, m, kind, ky] = len(slots)
    first["end"] = len(slots)
    return slots, first


SLOTS, FIRST = weight_slots()
NW = FIRST["end"]

ORDER = ["w15", "w13", "w25", "w12", "w23", "w22", "wd1", "wd2", "wd3"]
GROUP = {}
for _n in ORDER:
    for _h in range(2):
        GROUP[_n, _h] = len(GROUP)
for _m in range(3):
    for _h in range(2):
        GROUP["wca", _m, _h] = len(GROUP)
for _n in ("whf", "wcb"):
    for _h in range(2):
        GROUP[_n, _h] = len(GROUP)
NG = len(GROUP)
RING = 4
assert NG % RING == 0

COL = {n: i for i, n in enumerate(["b15", "b13", "b12", "b25", "b23", "b22", "bd1", "bd2", "bd3", "bca0", "bca1",
                                   "bca2", "bcb", "bn_gamma", "bn_beta", "bn_mean", "bn_var", "bhf"])}


def bank_turns():
    turns = []
    for c in range(XCHUNKS):
        turns.append(("ychunk", c))
        for t in range(c * CTILES, (c + 1) * CTILES):
            if t % CTILES == XTURN:
                turns.append(("xchunk", c))
            if t == TILES - 4:
                turns.append(("mean1",))
            if t == TILES - 2:
                turns.append(("var1",))
            turns.append(("tile", t))
    return turns


TURNS = bank_turns()
BANK = {x: i % BANKS for i, x in enumerate(TURNS)}
RUN_ENDS = [x[1] for x, y in zip(TURNS, TURNS[1:] + [("end",)]) if x[0] == "tile" and y[0] not in ("tile", "ychunk")]


def make_plan():
    plan = []
    for n in ORDER:
        for kind in KINDS[n]:
            for half in range(2):
                for m in maps_of(n, kind):
                    for ky in range(len(row_offsets(n, kind))):
                        plan.append(("mm", n, half, m, kind, ky))
    for m in range(3):
        for half in range(2):
            plan.append(("mm", "wca", half, m, OWN, 0))
    for m in range(4):
        if m == 3:
            plan += [("mm", "whf", half, 2, OWN, 0) for half in range(2)]
        for half in range(2):
            for ky in range(3):
                plan.append(("mm", "wcb", half, m, OWN, ky))
        if m in (1, 2):
            plan += [("mm", "whf", half, m - 1, OWN, 0) for half in range(2)]
        plan.append(("cbmap", m))
    for half in range(2):
        for kind in (LEFT, RIGHT):
            for ky in range(3):
                plan.append(("mm", "wcb", half, 0, kind, ky))
    at = {LEAD: [("mean2",)], LEAD + 4: [("var2",)], LEAD + 8: [("bias2",)], LEAD + 10: [("side",)]}
    places = [i for i in range(LEAD + 12, len(plan) - REAR)
              if not (plan[i][1] in ("w22", "wd1", "wd2", "wd3") and plan[i][4] != OWN and plan[i][2] == 1)]
    for k, x in enumerate(TURNS):
        at.setdefault(places[k * len(places) // len(TURNS)], []).append(x)
    out = []
    for i, x in enumerate(plan):
        out += at.get(i, [])
        out.append(x)
    return out


PLAN = make_plan()
MAKER = {"w25": "w15", "w23": "w13", "w22": "w12", "wd2": "wd1", "wd3": "wd2", "wca": "wd3"}
LEAKY = ORDER
HAS_EDGE = ["w15", "w13", "w12", "wd1", "wd2"]


def last_products():
    seen = {}
    for i, x in enumerate(PLAN):
        if x[0] == "mm":
            key = ("wca", x[3], x[2]) if x[1] == "wca" else (x[1], x[2])
            seen.setdefault(key, []).append(i)
    return {k: (v[0], v[-1]) for k, v in seen.items()}


SPAN = last_products()
MAP_DONE = [max(j for j in range(i) if PLAN[j][0] == "mm") for i, x in enumerate(PLAN) if x[0] == "cbmap"]


EDGES = ((slice(0, P // 2), slice(1, JN), slice(0, JN - 1)),
         (slice(P // 2, P), slice(0, JN - 1), slice(1, JN)))


SIDES = ((0, slice(P - CH, P), slice(0, JN - 1), slice(1, JN)),
         (1, slice(0, CH), slice(1, JN), slice(0, JN - 1)))


def wait(eng, sem, value):
    if not isinstance(value, int) or value > 0:
        eng.wait_ge(sem, value)


def wait_apart(eng, sem, value, passed):
    wait(eng, sem, value)
    eng.sem_inc(passed, 1)


def conv_vq_kernel(nc, x, weights, params, codes4, codebook, ident, group_mean, part_mask, out):
    ctx = ExitStack()
    with ctx:
        def sb(name, shape, dt=F32):
            return ctx.enter_context(nc.sbuf_tensor(name, shape, dt))

        def sem(name):
            return ctx.enter_context(nc.semaphore(name))

        w_sb = sb("w_sb", [P, NW, P])
        prm = sb("prm", [P, len(COL)])
        idn = sb("idn", [P, P])
        gmean = sb("gmean", [P, P])
        pmask = sb("pmask", [P, 4])
        cb4 = sb("cb4", [P, CODES])
        cbs = sb("cbs", [P, CODES])
        factors = sb("factors", [P, P])
        cst = sb("cst", [P, CODES], F32R)
        yh = sb("yh", [P, 2, 2, P], F32R)
        yl = sb("yl", [P, 2, 2, P], F32R)
        yst = sb("yst", [P, 2, BLK, 2, P], F32R)
        xnat = sb("xnat", [P, 2, CW])
        xord = sb("xord", [P, 2, CW])
        xt = sb("xt", [P, 2, 2, 2, 2, ROWS])
        sd = sb("sd", [P, 2, 2, 2, ROWS])
        chigh = xt[:, 0].rearrange("p w j e i -> p (w j e i)").bitcast(F32R)
        brest = sd[:, :].rearrange("p s j e i -> p (s j e i)")
        bands = [sb(f"bands{i}", [P, 2, JN, 2, ROWS]) for i in range(2)]
        hf = [[sb(f"hf{m}{k}", [P, JN, RP]) for k in range(2)] for m in range(3)]
        lln = sb("lln", [P, JN, RP])
        side = [sb(f"side{k}", [P, JN, RP]) for k in range(2)]
        ha = [sb(f"ha{k}", [P, JN, RP]) for k in range(2)]
        hb = [sb(f"hb{k}", [P, JN, RP]) for k in range(2)]
        br = [sb(f"br{m}", [P, JN, ROWS]) for m in range(3)]
        z = sb("z", [P, 2, HALF, ROWS])
        hsum = sb("hsum", [P, JN, ROWS])
        ync = sb("ync", [P, 2, CW])
        vqc = sb("vqc", [P, 2, CW])
        idx = sb("idx", [P, 2, 16, 8], U32)
        top8 = sb("top8", [P, 4, 8])
        st1 = sb("st1", [P, XCHUNKS, 6])
        st2 = sb("st2", [P, 4, 6])
        sth = sb("sth", [P, 4, 6])
        mvh = sb("mvh", [P, 2])
        hsq = sb("hsq", [P, 1])
        hvar = sb("hvar", [P, 1])
        vpart = sb("vpart", [P, 1])
        mv = [sb(f"mv{i}", [P, 2]) for i in range(2)]
        mall = [sb(f"mall{i}", [P, 1]) for i in range(2)]
        dev = [sb(f"dev{i}", [P, 1]) for i in range(2)]
        vsum = [sb(f"vsum{i}", [P, 1]) for i in range(2)]
        veps = [sb(f"veps{i}", [P, 1]) for i in range(2)]
        rstd = [sb(f"rstd{i}", [P, 1]) for i in range(2)]
        scale1 = sb("scale1", [P, 1])
        shift1 = sb("shift1", [P, 1])
        resid = [sb(f"resid{i}", [P, 1]) for i in range(2)]
        nresid = [sb(f"nresid{i}", [P, 1]) for i in range(2)]
        scale2 = sb("scale2", [P, 1])
        power = sb("power", [P, 1])
        folded = sb("folded", [P, 8])
        bnv, bnr, bns, bnt, bnb, bnsh, bnbh, bhfh = (folded[:, i:i + 1] for i in range(8))

        ring = [ctx.enter_context(nc.psum_tensor(f"ring{i}", [P, HALF, ROWS], F32)) for i in range(RING)]
        score = [ctx.enter_context(nc.psum_tensor(f"score{i}", [P, CODES], F32)) for i in range(4)]

        s_w = {n: sem(f"s_w_{n}") for n in CONVS}
        s_const = sem("s_const")
        s_zero = sem("s_zero")
        s_init = sem("s_init")
        s_x = [sem(f"s_x{i}") for i in range(2)]
        s_xT = sem("s_xT")
        s_xord = sem("s_xord")
        s_xev = sem("s_xev")
        s_dwt = sem("s_dwt")
        s_agg = [sem(f"s_agg{i}") for i in range(2)]
        s_mean = [sem(f"s_mean{i}") for i in range(2)]
        s_dev = [sem(f"s_dev{i}") for i in range(2)]
        s_var = [sem(f"s_var{i}") for i in range(2)]
        s_veps = [sem(f"s_veps{i}") for i in range(2)]
        s_rstd = [sem(f"s_rstd{i}") for i in range(2)]
        s_norm = sem("s_norm")
        s_lln = sem("s_lln")
        s_side = sem("s_side")
        s_hfw = sem("s_hfw")
        s_grp = sem("s_grp")
        s_free = sem("s_free")
        s_leaky = sem("s_leaky")
        s_edge = sem("s_edge")
        s_sum = sem("s_sum")
        s_phf = sem("s_phf")
        s_pside = sem("s_pside")
        s_cbmap = sem("s_cbmap")
        s_band = sem("s_band")
        s_de = sem("s_de")
        s_dl = sem("s_dl")
        s_neg = sem("s_neg")
        s_cbs = sem("s_cbs")
        s_bias = sem("s_bias")
        s_parts = sem("s_parts")
        s_yh = sem("s_yh")
        s_yl = sem("s_yl")
        s_yst = [sem(f"s_yst{i}") for i in range(2)]
        s_tile = sem("s_tile")
        s_idx = sem("s_idx")
        s_yT = sem("s_yT")
        s_yev = sem("s_yev")
        s_gather = [sem(f"s_gather{i}") for i in range(2)]
        s_add = sem("s_add")
        s_store = [sem(f"s_store{i}") for i in range(2)]
        s_yedge = sem("s_yedge")
        s_bnv = sem("s_bnv")
        s_bnr = sem("s_bnr")
        s_bn = sem("s_bn")
        s_passed = [sem(f"s_passed{i}") for i in range(3)]
        s_top = sem("s_top")
        s_d0, s_dn, s_dc, s_dq = (sem(n) for n in ("s_d0", "s_dn", "s_dc", "s_dq"))

        LEAKY_TILE = {"w15": ha, "w13": hb, "w12": ha, "wd1": ha, "wd2": hb, "wd3": ha}

        block = ctx.enter_context(nc.Block())
        xv = x.rearrange("b (i e) w c -> b e i (w c)", e=2)
        ov = out.rearrange("b (i e) w c -> b e i (w c)", e=2)

        def rounds(eng, body):
            body(0, 0, True, False, True)
            with eng.Fori(0, (IMAGES - 2) // 2) as i:
                body(2 * i + 1, 1, True, True, True)
                body(2 * i + 2, 0, True, True, True)
            body(IMAGES - 1, 1, True, True, False)
            body(IMAGES, 0, False, True, False)

        def own(tile, half, rows=slice(PAD, PAD + ROWS)):
            return tile[:, half * HALF:(half + 1) * HALF, rows]

        def raw(par, slot):
            return bands[par][:, slot // 2, :, slot % 2, :]

        @block.sync
        def _(sp):
            def load(b, k):
                wait(sp, s_xord, XCHUNKS * b + k - 1)
                for e in range(2):
                    sp.dma_start(xnat[e * ROWS:(e + 1) * ROWS, k % 2, :],
                                 xv[b, e, :, k * CW:(k + 1) * CW] if isinstance(b, int) else
                                 xv[bass.ds(b, 1), e, :, k * CW:(k + 1) * CW].rearrange("b i n -> (b i) n")
                                 ).then_inc(s_x[k % 2], 16)

            def store(v, c):
                sp.wait_ge(s_add, PRIMED + XCHUNKS * v + c + 1)
                for e in range(2):
                    sp.dma_start(ov[v, e, :, c * CW:(c + 1) * CW] if isinstance(v, int) else
                                 ov[bass.ds(v, 1), e, :, c * CW:(c + 1) * CW].rearrange("b i n -> (b i) n"),
                                 vqc[e * ROWS:(e + 1) * ROWS, c % 2, :]).then_inc(s_store[c % 2], 16)

            for dst, src in ((idn, ident), (gmean, group_mean), (prm, params), (cb4, codes4), (pmask, part_mask)):
                sp.dma_start(dst[:, :], src[:, :]).then_inc(s_const, 16)
            for k in range(XCHUNKS):
                load(0, k)

            def stack(v, j):
                if j >= 2:
                    wait_apart(sp, s_tile, TILES * v + JTILES * (j - 1), s_passed[2])
                sp.wait_ge(s_yl, JN * v + j + 1)
                for k, part in enumerate((yh, yl, yh)):
                    for g in range(BLK):
                        sp.dma_start(yst[k * CH:(k + 1) * CH, j % 2, g].bitcast(F32),
                                     part[g * CH:(g + 1) * CH, j % 2].bitcast(F32)).then_inc(s_yst[j % 2], 16)

            def body(b, par, conv, quant, nxt):
                early = 4 if quant else XCHUNKS
                if nxt:
                    for k in range(early):
                        load(b + 1, k)
                if quant:
                    for j in range(JN):
                        stack(b - 1, j)
                        if j >= 4 and j % 2 == 0:
                            store(b - 1, j // 2 - 2)
                        if nxt and j % 2 and early <= j // 2 + 3 < XCHUNKS:
                            load(b + 1, j // 2 + 3)
                    for c in range(XCHUNKS - 2, XCHUNKS):
                        store(b - 1, c)

            rounds(sp, body)
            for i in range(2):
                sp.wait_ge(s_store[i], PRIMED + 32 * (XCHUNKS // 2) * IMAGES)

        @block.tensor
        def _(pe):
            def transpose4(dst, src, last):
                for n in range(4):
                    t = nc.tensor.transpose(dst[:, n * P:(n + 1) * P], src(n), idn[:, :])
                t.then_inc(last, 1)

            def bank_free(v, turn, quant, nxt):
                u = TURNS.index(turn) - BANKS
                while u >= 0:
                    what, k = TURNS[u][0], TURNS[u][-1]
                    if what == "xchunk" and nxt:
                        pe.wait_ge(s_xev, XCHUNKS * (v + 2) + k + 1)
                        return
                    if what == "ychunk" and quant:
                        pe.wait_ge(s_yev, XCHUNKS * v + k + 1)
                        return
                    if what == "tile" and quant:
                        pe.wait_ge(s_idx, TILES * v + k + 1)
                        return
                    if what in ("mean1", "var1") and nxt:
                        pe.wait_ge((s_dev if what == "mean1" else s_veps)[0], v + 3)
                        return
                    u -= BANKS
                if quant:
                    pe.wait_ge(s_parts, v + 1)

            def xchunk(b, k, bank):
                pe.wait_ge(s_xord, XCHUNKS * b + k + 1)
                transpose4(score[bank], lambda n: xord[:, k % 2, n * P:(n + 1) * P], s_xT)

            def combine(which, src, bank, ready, n, done):
                pe.wait_ge(ready, n + 1)
                nc.tensor.matmul(score[bank][:, 0:1], gmean[:, :], src, start=True, stop=True).then_inc(done, 1)

            def mean(which, n, bank):
                combine(which, mv[which][:, 0:1], bank, s_agg[which], n, s_mean[which])

            def var(which, n, bank):
                combine(which, vsum[which][:, :], bank, s_dev[which], n, s_var[which])

            def bias2(v):
                pe.wait_ge(s_neg, v + 1)
                pe.wait_ge(s_cbs, v + 1)
                nc.tensor.matmul(score[2][:, :], factors[:, :], cbs[:, :], start=True, stop=True)\
                    .then_inc(s_bias, 1)

            def yview(par, wp, j):
                return bands[par][:, wp, j].rearrange("p e i -> p (e i)")

            def ychunk(v, par, c):
                transpose4(score[BANK["ychunk", c]], lambda n: yview(par, n % 2, 2 * c + n // 2), s_yT)

            def tile(v, t):
                j = t // JTILES
                if t % JTILES == 0:
                    pe.wait_ge(s_yst[j % 2], STACKED * ((JN // 2) * v + j // 2 + 1))
                wp, g = t % JTILES // BLK, t % BLK
                nc.tensor.matmul(score[BANK["tile", t]][:, :], yst[0:KST, j % 2, g, wp], cst[0:KST, :],
                                 start=True, stop=True).then_inc(s_tile, 1)

            def source(n, m, kind):
                if kind in (LEFT, RIGHT):
                    return side[kind - LEFT]
                if n == "wcb" and m == 0:
                    return lln
                if n == "wcb":
                    return hf[m - 1][0]
                if n in ("w15", "w13", "w12", "whf"):
                    return hf[m][kind]
                return {"w25": ha, "w23": hb, "w22": ha, "wd1": hb, "wd2": ha, "wd3": hb, "wca": ha}[n][kind]

            def inputs_ready(b, n, half, m, kind):
                if n == "w15" and half == 0:
                    pe.wait_ge(s_hfw, 6 * b + (m + 1 if kind == 0 else m + 4))
                elif n == "w13" and kind == LEFT and half == 0:
                    pe.wait_ge(s_side, b + 1)
                elif n in MAKER and m == 0:
                    if kind == 0:
                        pe.wait_ge(s_leaky, len(LEAKY) * 2 * b + GROUP[MAKER[n], half] + 1)
                    elif half == 0:
                        pe.wait_ge(s_edge, len(HAS_EDGE) * b + HAS_EDGE.index(MAKER[n]) + 1)
                elif n == "wd1":
                    if kind == 0:
                        pe.wait_ge(s_sum, 2 * b + half + 1)
                    elif half == 0:
                        pe.wait_ge(s_yedge, b + 1)
                elif n == "wcb":
                    if kind != OWN:
                        if kind == LEFT and half == 0:
                            pe.wait_ge(s_pside, b + 1)
                    elif m == 0:
                        if half == 0:
                            pe.wait_ge(s_lln, b + 1)
                    else:
                        pe.wait_ge(s_phf, 6 * b + 2 * (m - 1) + half + 1)
                elif n == "whf" and m == 2:
                    pe.wait_ge(s_phf, 6 * b + 2 * m + half + 1)

            def product(i, b, n, half, m, kind, ky, seen):
                key = ("wca", m, half) if n == "wca" else (n, half)
                first, last = SPAN[key]
                g = GROUP[key]
                if i == first:
                    wait(pe, s_free, NG * b + g - (RING - 1))
                if (n, half, m, kind) not in seen:
                    seen.add((n, half, m, kind))
                    if isinstance(b, int) and b == 0 and ("w", n) not in seen:
                        seen.add(("w", n))
                        pe.wait_ge(s_w[n], 16)
                    inputs_ready(b, n, half, m, kind)
                di = row_offsets(n, kind)[ky]
                t = nc.tensor.matmul(ring[g % RING][:, :, :], w_sb[:, SLOTS[n, m, kind, ky], :],
                                     own(source(n, m, kind), half, slice(PAD + di, PAD + di + ROWS)),
                                     start=(i == first), stop=(i == last))
                if i == last:
                    t.then_inc(s_grp, 1)
                elif i in MAP_DONE:
                    t.then_inc(s_cbmap, 1)

            def body(b, par, conv, quant, nxt):
                seen, v = set(), b - 1
                for i, step in enumerate(PLAN):
                    what = step[0]
                    if what == "mm" and conv:
                        product(i, b, *step[1:], seen)
                    elif quant and what == "mean2":
                        wait(pe, s_veps[0], b + 1 if conv else b)
                        wait(pe, s_idx, TILES * v)
                        mean(1, v, 0)
                    elif quant and what == "var2":
                        var(1, v, 1)
                    elif quant and what == "bias2":
                        bias2(v)
                    elif quant and what == "ychunk":
                        bank_free(v, step, quant, nxt)
                        ychunk(v, 1 - par, step[1])
                    elif quant and what == "tile":
                        bank_free(v, step, quant, nxt)
                        tile(v, step[1])
                    elif nxt and what == "xchunk":
                        bank_free(v, step, quant, nxt)
                        xchunk(b + 1, step[1], BANK[step])
                    elif nxt and what == "mean1":
                        bank_free(v, step, quant, nxt)
                        mean(0, b + 1, BANK[step])
                    elif nxt and what == "var1":
                        bank_free(v, step, quant, nxt)
                        var(0, b + 1, BANK[step])

            pe.wait_ge(s_const, 16 * 5)
            pe.wait_ge(s_init, 1)
            for k in range(XCHUNKS):
                if k >= BANKS:
                    pe.wait_ge(s_xev, k - BANKS + 1)
                xchunk(0, k, k % BANKS)
            mean(0, 0, 0)
            var(0, 0, 1)
            rounds(pe, body)

        @block.scalar
        def _(act):
            for n in CONVS:
                hi = min([f for f in FIRST.values() if f > FIRST[n]])
                act.dma_start(w_sb[:, FIRST[n]:hi, :], weights[:, FIRST[n]:hi, :]).then_inc(s_w[n], 16)

            def col(name):
                return prm[:, COL[name]:COL[name] + 1]

            def edge_copy(tiles):
                for p, src, dst in EDGES:
                    t = nc.scalar.copy(tiles[1][p, dst, PAD:PAD + ROWS], tiles[0][p, src, PAD:PAD + ROWS])
                return t

            def packed_copy(tiles, both):
                near = (0, 3) if both else (0,)
                for group in near:
                    src, dst = EDGES[group // 2][1:]
                    for shift in range(2):
                        to = abs(group - shift)
                        t = nc.scalar.copy(tiles[1][to * CH:(to + 1) * CH, dst, PAD:PAD + ROWS],
                                           tiles[0][group * CH:(group + 1) * CH, src,
                                                    PAD + shift:PAD + shift + ROWS])
                return t

            def evacuate(b, key):
                g = GROUP[key]
                n, half = key[0], key[-1]
                bank = ring[g % RING]
                act.wait_ge(s_grp, NG * b + g + 1)
                if n in LEAKY:
                    wait(act, s_leaky, len(LEAKY) * 2 * b + g - 1)
                    nc.scalar.activation(z[:, g % 2], bank[:, :, :], ACT.Identity, bias=col("b" + n[1:]))\
                        .then_inc(s_free, 1)
                    if half == 1 and n in HAS_EDGE:
                        act.wait_ge(s_leaky, len(LEAKY) * 2 * b + g + 1)
                        fill = packed_copy(LEAKY_TILE[n], n == "w13") if n in ("w13", "w12") else \
                            edge_copy(LEAKY_TILE[n])
                        fill.then_inc(s_edge, 1)
                    if half == 1 and n == "w22":
                        act.wait_ge(s_sum, 2 * b + 2)
                        edge_copy(hb).then_inc(s_yedge, 1)
                elif n == "wca":
                    m = key[1]
                    nc.scalar.activation(br[m][:, half * HALF:(half + 1) * HALF, :], bank[:, :, :],
                                         ACT.Sigmoid, bias=col(f"bca{m}")).then_inc(s_free, 1)
                elif n == "whf":
                    t = nc.scalar.activation(br[2][:, half * HALF:(half + 1) * HALF, :], bank[:, :, :],
                                             ACT.Identity, bias=bhfh[:, :], scale=0.5)
                    t.then_inc(s_free, 1)
                else:
                    nc.scalar.activation(br[0][:, half * HALF:(half + 1) * HALF, :], bank[:, :, :],
                                         ACT.Identity, bias=bnbh[:, :], scale=bnsh[:, :])
                    t = nc.scalar.activation(br[1][:, half * HALF:(half + 1) * HALF, :], bank[:, :, :],
                                             ACT.Sigmoid, bias=bnb[:, :], scale=bns[:, :])
                    t.then_inc(s_free, 1)

            def high(v, par, j):
                act.wait_ge(s_band, v + 1)
                if j >= 2:
                    act.wait_ge(s_yst[j % 2], STACKED * ((JN // 2) * v + j // 2))
                nc.scalar.copy(yh[:, j % 2], bands[par][:, :, j].rearrange("p w e i -> p w (e i)"))\
                    .then_inc(s_yh, 1)

            def weighted_sides(b):
                for k in range(3):
                    act.wait_ge(s_phf, 6 * b + 2 * k + 2)
                    for to, near, src, dst in SIDES:
                        t = nc.scalar.copy(side[to][k * CH:(k + 1) * CH, dst, PAD:PAD + ROWS],
                                           hf[k][0][near, src, PAD:PAD + ROWS])
                t.then_inc(s_pside, 1)

            def xorder(b, k):
                act.wait_ge(s_x[k % 2], 32 * ((XCHUNKS // 2) * b + k // 2 + 1))
                wait(act, s_xT, XCHUNKS * b + k - 1)
                src = xnat[:, k % 2, :].rearrange("p (j g w c) -> p w j g c", g=4, w=2, c=CH)
                dst = xord[:, k % 2, :].rearrange("p (w j g c) -> p w j g c", w=2, g=4, c=CH)
                for w in range(2):
                    t = nc.scalar.copy(dst[:, w], src[:, w])
                t.then_inc(s_xord, 1)

            def xcopy(b, k, bank):
                if k + 2 < XCHUNKS:
                    xorder(b, k + 2)
                act.wait_ge(s_xT, XCHUNKS * b + k + 1)
                wait(act, s_dwt, XCHUNKS * b + k - 1)
                nc.scalar.copy(xt[:, k % 2].rearrange("p w j e i -> p (w j e i)"), score[bank][:, :])\
                    .then_inc(s_xev, 1)

            def ycopy(v, c):
                act.wait_ge(s_yT, XCHUNKS * v + c + 1)
                act.wait_ge(s_add, PRIMED + XCHUNKS * v + max(c - 1, 0))
                dst = ync[:, c % 2, :].rearrange("p (j g w c) -> p j w g c", g=4, w=2, c=CH)
                src = score[BANK["ychunk", c]][:, :].rearrange("p (j w g c) -> p j w g c", g=4, w=2, c=CH)
                for j in range(2):
                    t = nc.scalar.copy(dst[:, j], src[:, j])
                t.then_inc(s_yev, 1)

            def normal_ll(n, par):
                wait(act, s_cbmap, 4 * (n - 1) + 1)
                nc.scalar.activation(lln[:, :, PAD:PAD + ROWS], raw(par, LL), ACT.Identity, bias=shift1[:, :],
                                     scale=scale1[:, :]).then_inc(s_lln, 1)

            def normal_own(n, par, m):
                act.wait_ge(s_norm, n + 1)
                wait(act, s_cbmap, 4 * (n - 1) + m + 2)
                nc.scalar.activation(hf[m][0][:, :, PAD:PAD + ROWS], raw(par, BANDS[m]), ACT.Identity,
                                     bias=0.0, scale=scale1[:, :]).then_inc(s_hfw, 1)

            def normal_side(n, par):
                for to, near, src, dst in SIDES:
                    for q in range(4):
                        band = raw(par, LL if q == SIDE_LL else BANDS[q])
                        t = nc.scalar.activation(side[to][q * CH:(q + 1) * CH, dst, PAD:PAD + ROWS],
                                                 band[near, src], ACT.Identity,
                                                 bias=shift1[near, :] if q == SIDE_LL else 0.0,
                                                 scale=scale1[near, :])
                t.then_inc(s_side, 1)

            def normal_edge(n, par, m):
                for p, s, d in EDGES:
                    t = nc.scalar.activation(hf[m][1][p, d, PAD:PAD + ROWS], raw(par, BANDS[m])[p, s],
                                             ACT.Identity, bias=0.0, scale=scale1[p, :])
                t.then_inc(s_hfw, 1)

            def body(b, par, conv, quant, nxt):
                v = b - 1
                for i, step in enumerate(PLAN):
                    what = step[0]
                    if nxt and i == 0:
                        for k in range(2):
                            xorder(b + 1, k)
                    if quant and what == "mean2":
                        for j in range(2):
                            high(v, 1 - par, j)
                    elif quant and what == "tile":
                        if step[1] % JTILES == JTILES // 2 and step[1] // JTILES + 2 < JN:
                            high(v, 1 - par, step[1] // JTILES + 2)
                    elif quant and what == "ychunk":
                        ycopy(v, step[1])
                    elif nxt and what == "xchunk":
                        xcopy(b + 1, step[1], BANK[step])
                    elif nxt and what == "cbmap" and step[1] == 3:
                        for m in range(3):
                            normal_own(b + 1, 1 - par, m)
                        normal_ll(b + 1, 1 - par)
                    elif conv and what == "side":
                        normal_side(b, par)
                    elif conv and what == "cbmap" and step[1] == 1:
                        weighted_sides(b)
                    elif conv and what == "mm":
                        for key, (_, last) in SPAN.items():
                            if last == i:
                                evacuate(b, key)
                if nxt:
                    for m in range(3):
                        normal_edge(b + 1, 1 - par, m)

            act.wait_ge(s_zero, 1)
            act.wait_ge(s_bn, 1)
            for k in range(2):
                xorder(0, k)
            for k in range(XCHUNKS):
                xcopy(0, k, k % BANKS)
            for m in range(3):
                normal_own(0, 0, m)
            normal_ll(0, 0)
            for m in range(3):
                normal_edge(0, 0, m)
            rounds(act, body)

        @block.vector
        def _(dve):
            def after(ins, sem, value):
                ins.then_inc(sem, 1)
                dve.wait_ge(sem, value)

            def statistics(which, n, sem, base, bank, variances):
                dve.wait_ge(s_mean[which], n + 1)
                after(nc.vector.tensor_copy(mall[which][:, :], score[bank][:, 0:1]), sem, base + 1)
                after(nc.vector.tensor_tensor(dev[which][:, :], mv[which][:, 0:1], mall[which][:, :],
                                              ALU.subtract), sem, base + 2)
                nc.vector.scalar_tensor_tensor(out=vsum[which][:, :], in0=dev[which][:, :],
                                               scalar=dev[which][:, :], in1=variances, op0=ALU.mult,
                                               op1=ALU.add).then_inc(s_dev[which], 1)

            def variance(which, n, bank):
                dve.wait_ge(s_var[which], n + 1)
                nc.vector.tensor_scalar_add(veps[which][:, :], score[bank][:, 0:1], GN_EPS).then_inc(s_veps[which], 1)
                dve.wait_ge(s_rstd[which], n + 1)

            NSTEP = 2 * XCHUNKS + 5

            def xchunk(n, par, k):
                base = NSTEP * n + 2 * k
                dve.wait_ge(s_xev, XCHUNKS * n + k + 1)
                slot = xt[:, k % 2]
                nc.vector.bn_stats(st1[:, k, :], slot.rearrange("p w j e i -> p (w j e i)"))
                wait(dve, s_dwt, XCHUNKS * n + k)
                nc.vector.tensor_tensor(sd[:, 0], slot[:, 0], slot[:, 1], ALU.add).then_inc(s_dn, 1)
                nc.vector.tensor_tensor(sd[:, 1], slot[:, 1], slot[:, 0], ALU.subtract).then_inc(s_dn, 1)
                dve.wait_ge(s_dn, base + 2)
                js = slice(2 * k, 2 * k + 2)
                pair = sd[:, :].rearrange("p s j e i -> p e j s i")
                nc.vector.tensor_tensor(bands[par][:, 0, js], pair[:, 0], pair[:, 1], ALU.add)
                nc.vector.tensor_tensor(bands[par][:, 1, js], pair[:, 1], pair[:, 0], ALU.subtract)\
                    .then_inc(s_dwt, 1)

            def aggregate1(n):
                wait_apart(dve, s_dwt, XCHUNKS * (n + 1), s_passed[0])
                nc.vector.bn_aggr(mv[0][:, :], st1[:, :, :]).then_inc(s_agg[0], 1)

            def mean1(n, bank):
                statistics(0, n, s_dn, NSTEP * n + 2 * XCHUNKS, bank, mv[0][:, 1:2])

            def var1(n, par, bank):
                variance(0, n, bank)
                wait(dve, s_side, n)
                nc.vector.tensor_scalar_mul(scale1[:, :], rstd[0][:, :], 0.5).then_inc(s_dn, 1)
                nc.vector.tensor_scalar(resid[par][:, :], rstd[0][:, :], 0.25, 0.25, ALU.mult, ALU.add)\
                    .then_inc(s_dn, 1)
                nc.vector.tensor_scalar(nresid[par][:, :], rstd[0][:, :], -0.25, -0.25, ALU.mult, ALU.add)\
                    .then_inc(s_dn, 1)
                dve.wait_ge(s_dn, NSTEP * (n + 1))
                nc.vector.tensor_scalar(shift1[:, :], mall[0][:, :], rstd[0][:, :], -2.0, ALU.mult, ALU.mult)\
                    .then_inc(s_norm, 1)

            def leaky(b, n, half):
                g = GROUP[n, half]
                js = slice(half * HALF, (half + 1) * HALF)
                dst = own(LEAKY_TILE[n][0], half) if n in LEAKY_TILE else br[("w25", "w23", "w22").index(n)][:, js, :]
                dve.wait_ge(s_free, NG * b + g + 1)
                nc.vector.scalar_tensor_tensor(out=dst, in0=z[:, g % 2], scalar=LEAK, in1=z[:, g % 2],
                                               op0=ALU.mult, op1=ALU.max).then_inc(s_leaky, 1)

            def branch_sum(b, half):
                js = slice(half * HALF, (half + 1) * HALF)
                dve.wait_ge(s_leaky, len(LEAKY) * 2 * b + GROUP["w22", half] + 1)
                after(nc.vector.tensor_tensor(br[0][:, js, :], br[0][:, js, :], br[1][:, js, :], ALU.add),
                      s_dc, 2 * b + half + 1)
                nc.vector.tensor_tensor(own(hb[0], half), br[0][:, js, :], br[2][:, js, :], ALU.add)\
                    .then_inc(s_sum, 1)

            ESTEP, LSTEP, QSTEP = 6, 4, 2 + 2 + 1 + 3

            def upper_bands(b, par):
                base = ESTEP * b
                dve.wait_ge(s_side, b + 1)
                after(nc.vector.tensor_tensor(hsum[:, :, :], raw(par, HL), raw(par, HH), ALU.add), s_de, base + 1)
                after(nc.vector.tensor_tensor(raw(par, HH), raw(par, HL), raw(par, HH), ALU.subtract),
                      s_de, base + 2)
                for h in range(2):
                    js = slice(h * HALF, (h + 1) * HALF)
                    nc.vector.bn_stats(sth[:, h, :], hsum[:, js, :].rearrange("p j i -> p (j i)"))
                    t = nc.vector.bn_stats(sth[:, 2 + h, :], raw(par, HH)[:, js])
                t.then_inc(s_de, 1)
                wait_apart(dve, s_de, base + 3, s_passed[0])
                after(nc.vector.bn_aggr(mvh[:, :], sth[:, :, :]), s_de, base + 4)
                after(nc.vector.scalar_tensor_tensor(out=hsq[:, :], in0=mvh[:, 0:1], scalar=mvh[:, 0:1],
                                                     in1=mvh[:, 1:2], op0=ALU.mult, op1=ALU.add), s_de, base + 5)
                nc.vector.tensor_scalar(hvar[:, :], hsq[:, :], resid[par][:, :], resid[par][:, :],
                                        ALU.mult, ALU.mult).then_inc(s_de, 1)
                dve.wait_ge(s_free, NG * b + GROUP["whf", 1] + 1)
                nc.vector.scalar_tensor_tensor(out=raw(par, LH), in0=raw(par, LH), scalar=0.25, in1=br[2][:, :, :],
                                               op0=ALU.mult, op1=ALU.add)

            def lower_bands(b, par, half):
                js = slice(half * HALF, (half + 1) * HALF)
                base = LSTEP * (2 * b + half)
                low, high = raw(par, LL)[:, js], raw(par, LH)[:, js]
                dve.wait_ge(s_free, NG * b + GROUP["wcb", half] + 1)
                after(nc.vector.tensor_tensor(br[0][:, js, :], br[0][:, js, :], br[1][:, js, :], ALU.mult),
                      s_dl, base + 1)
                after(nc.vector.scalar_tensor_tensor(out=low, in0=low, scalar=0.25, in1=br[0][:, js, :],
                                                     op0=ALU.mult, op1=ALU.add), s_dl, base + 2)
                nc.vector.tensor_tensor(z[:, half], low, high, ALU.add)
                after(nc.vector.tensor_tensor(raw(par, HL)[:, js], low, high, ALU.subtract), s_dl, base + 3)
                nc.vector.bn_stats(st2[:, half, :], z[:, half].rearrange("p j i -> p (j i)"))
                nc.vector.bn_stats(st2[:, 2 + half, :], raw(par, HL)[:, js]).then_inc(s_dl, 1)

            def finish(v, par):
                base = QSTEP * v
                wait_apart(dve, s_dl, LSTEP * 2 * (v + 1), s_passed[0])
                nc.vector.bn_aggr(mv[1][:, :], st2[:, :, :]).then_inc(s_agg[1], 1)
                for out_lh, res in ((raw(par, LL), nresid), (raw(par, LH), resid)):
                    t = nc.vector.scalar_tensor_tensor(out=out_lh, in0=raw(par, HH), scalar=res[par][:, :],
                                                       in1=raw(par, HL), op0=ALU.mult, op1=ALU.add)
                after(t, s_dq, base + 1)
                for out_h, res in ((raw(par, HL), nresid), (raw(par, HH), resid)):
                    t = nc.vector.scalar_tensor_tensor(out=out_h, in0=hsum[:, :, :], scalar=res[par][:, :],
                                                       in1=z[:, :].rearrange("p h j i -> p (h j) i"),
                                                       op0=ALU.mult, op1=ALU.add)
                t.then_inc(s_band, 1)
                dve.wait_ge(s_agg[1], v + 1)
                after(nc.vector.tensor_tensor(vpart[:, :], mv[1][:, 1:2], hvar[:, :], ALU.add), s_dq, base + 2)

            def var2(v):
                variance(1, v, 1)
                base = QSTEP * v + 4
                after(nc.vector.tensor_scalar_mul(scale2[:, :], rstd[1][:, :], 2.0), s_dq, base + 1)
                nc.vector.tensor_scalar(factors[0:CH, :], idn[0:CH, :], 0.0, mall[1][0:CH, :],
                                        ALU.mult, ALU.subtract).then_inc(s_neg, 1)
                nc.vector.tensor_scalar(cbs[0:3 * CH, :], cb4[0:3 * CH, :], scale2[0:3 * CH, :], None, ALU.mult)\
                    .then_inc(s_cbs, 1)

            def bias2(v):
                base = QSTEP * v + 5
                hh, lo, bb = slice(0, 2 * CH), slice(2 * CH, 3 * CH), slice(3 * CH, KST)
                dve.wait_ge(s_cbs, v + 1)
                nc.vector.tensor_copy(cst[hh, :], cbs[hh, :])
                after(nc.vector.tensor_copy(chigh[lo, :], cbs[lo, :]), s_dq, base + 1)
                nc.vector.tensor_tensor(cst[lo, :], cbs[lo, :], chigh[lo, :], ALU.subtract)
                dve.wait_ge(s_bias, v + 1)
                after(nc.vector.tensor_copy(chigh[bb, :], score[2][bb, :]), s_dq, base + 2)
                after(nc.vector.scalar_tensor_tensor(out=brest[bb, :], in0=chigh[bb, :], scalar=pmask[bb, 0:1],
                                                     in1=score[2][bb, :], op0=ALU.mult, op1=ALU.add),
                      s_dq, base + 3)
                nc.vector.tensor_copy(cst[bb, :], brest[bb, :]).then_inc(s_parts, 1)

            def maximum(v, t):
                if t % CTILES == 0:
                    c = t // CTILES
                    dve.wait_ge(s_add, PRIMED + XCHUNKS * v + max(c - 1, 0))
                wait_apart(dve, s_tile, TILES * v + t + 1, s_passed[0])
                nc.vector.max(top8[:, t % 4, :], score[BANK["tile", t]][:, :]).then_inc(s_top, 1)

            def index(v, t):
                wait_apart(dve, s_top, TILES * v + t + 1, s_passed[0])
                nc.vector.max_index(idx[:, t // CTILES % 2, t % CTILES, :], top8[:, t % 4, :],
                                    score[BANK["tile", t]][:, :]).then_inc(s_idx, 1)

            def body(b, par, conv, quant, nxt):
                v = b - 1
                pending = None
                if quant:
                    finish(v, 1 - par)
                for i, step in enumerate(PLAN):
                    what = step[0]
                    if quant and what == "mean2":
                        statistics(1, v, s_dq, QSTEP * v + 2, 0, vpart[:, :])
                    elif quant and what == "var2":
                        var2(v)
                    elif quant and what == "bias2":
                        bias2(v)
                    elif quant and what == "tile":
                        t = step[1]
                        maximum(v, t)
                        if pending is not None:
                            index(v, pending)
                        pending = t
                        if t in RUN_ENDS:
                            index(v, t)
                            pending = None
                    elif nxt and what == "xchunk":
                        xchunk(b + 1, 1 - par, step[1])
                        if step[1] == XCHUNKS - 1:
                            aggregate1(b + 1)
                    elif nxt and what == "mean1":
                        mean1(b + 1, BANK[step])
                    elif nxt and what == "var1":
                        var1(b + 1, 1 - par, BANK[step])
                    elif conv and what == "cbmap" and step[1] == 3:
                        upper_bands(b, par)
                    elif conv and what == "mm" and step[1] == "wcb" and SPAN["wcb", step[2]][1] == i:
                        lower_bands(b, par, step[2])
                    elif conv and what == "mm":
                        n, half = step[1], step[2]
                        if n in LEAKY and SPAN[n, half][1] == i:
                            leaky(b, n, half)
                            if n == "w22":
                                branch_sum(b, half)

            squares = slice(3 * CH, P)
            nc.vector.memset(factors[0:3 * CH, :], 0.0)
            nc.vector.memset(yst[3 * CH:KST].bitcast(F32).rearrange("p s g w n -> p (s g w n)"), 1.0)
            nc.vector.memset(factors[squares, :], -1.0).then_inc(s_init, 1)
            dve.wait_ge(s_const, 16 * 5)
            after(nc.vector.tensor_tensor(cbs[squares, :], cb4[squares, :], cb4[squares, :], ALU.mult), s_d0, 1)

            def col(name):
                return prm[:, COL[name]:COL[name] + 1]

            nc.vector.tensor_scalar_add(bnv[:, :], col("bn_var"), BN_EPS).then_inc(s_bnv, 1)
            dve.wait_ge(s_bnr, 1)
            after(nc.vector.tensor_tensor(bns[:, :], bnr[:, :], col("bn_gamma"), ALU.mult), s_d0, 2)
            after(nc.vector.tensor_tensor(bnt[:, :], col("bcb"), col("bn_mean"), ALU.subtract), s_d0, 3)
            after(nc.vector.scalar_tensor_tensor(out=bnb[:, :], in0=bnt[:, :], scalar=bns[:, :],
                                                 in1=col("bn_beta"), op0=ALU.mult, op1=ALU.add), s_d0, 4)
            nc.vector.tensor_scalar_mul(bnsh[:, :], bns[:, :], 0.5)
            nc.vector.tensor_scalar_mul(bnbh[:, :], bnb[:, :], 0.5)
            nc.vector.tensor_scalar_mul(bhfh[:, :], col("bhf"), 0.5).then_inc(s_bn, 1)
            for k in range(XCHUNKS):
                xchunk(0, 0, k)
            aggregate1(0)
            mean1(0, 0)
            var1(0, 0, 1)
            rounds(dve, body)

        @block.gpsimd
        def _(pool):
            def rsqrt(dst, src, done):
                nc.gpsimd.tensor_tensor(dst[:, :], src[:, :], power[:, :], ALU.pow).then_inc(done, 1)

            def norm(which, n):
                pool.wait_ge(s_veps[which], n + 1)
                rsqrt(rstd[which], veps[which], s_rstd[which])

            def gather(v, t):
                c, k = t // CTILES, t % CTILES
                if k == 0:
                    pool.wait_ge(s_store[c % 2], PRIMED + 32 * ((XCHUNKS // 2) * v + c // 2))
                wait_apart(pool, s_idx, TILES * v + t + 1, s_passed[1])
                w = 8 * (k // JTILES) + 2 * (k % BLK) + k % JTILES // BLK
                nc.gpsimd.indirect_dma_start(
                    vqc[:, c % 2, w * CH:(w + 1) * CH], None, codebook[:, :],
                    bass.IndirectOffsetOnAxis(idx[:, c % 2, k, 0:1], 0)).then_inc(s_gather[c % 2], 16)

            def low(v, par, j):
                pool.wait_ge(s_yh, JN * v + j + 1)
                nc.gpsimd.tensor_tensor(yl[:, j % 2], bands[par][:, :, j].rearrange("p w e i -> p w (e i)"),
                                        yh[:, j % 2], ALU.subtract).then_inc(s_yl, 1)

            def add(v, c):
                pool.wait_ge(s_yev, XCHUNKS * v + c + 1)
                pool.wait_ge(s_gather[c % 2], 256 * ((XCHUNKS // 2) * v + c // 2 + 1))
                nc.gpsimd.tensor_tensor(vqc[:, c % 2, :], vqc[:, c % 2, :], ync[:, c % 2, :], ALU.add)\
                    .then_inc(s_add, 1)

            def attend(b, m):
                for half in range(2):
                    js = slice(half * HALF, (half + 1) * HALF)
                    pool.wait_ge(s_free, NG * b + GROUP["wca", m, half] + 1)
                    nc.gpsimd.tensor_tensor(own(hf[m][0], half), own(hf[m][0], half), br[m][:, js, :], ALU.mult)\
                        .then_inc(s_phf, 1)

            def body(b, par, conv, quant, nxt):
                v = b - 1
                for i, step in enumerate(PLAN):
                    what = step[0]
                    if quant and what == "mean2":
                        for j in range(2):
                            low(v, 1 - par, j)
                    elif quant and what == "var2":
                        norm(1, v)
                    elif quant and what == "tile":
                        t = step[1]
                        if t % JTILES == JTILES // 2 and t // JTILES + 2 < JN:
                            low(v, 1 - par, t // JTILES + 2)
                        gather(v, t)
                        if t % CTILES == 5 and t > CTILES:
                            add(v, t // CTILES - 1)
                    elif nxt and what == "var1":
                        norm(0, b + 1)
                    elif conv and what == "mm":
                        for m in range(3):
                            if SPAN["wca", m, 1][1] == i:
                                attend(b, m)
                if quant:
                    add(v, XCHUNKS - 1)

            for counter in (s_add, *s_store):
                pool.sem_inc(counter, PRIMED)
            nc.gpsimd.memset(power[:, :], -0.5)
            tiles = [t for pair in (*hf, (lln,), side, ha, hb) for t in pair]
            for t in tiles:
                last = nc.gpsimd.memset(t[:, :, :], 0.0)
            last.then_inc(s_zero, 1)
            pool.wait_ge(s_zero, 1)
            pool.wait_ge(s_bnv, 1)
            rsqrt(bnr, bnv, s_bnr)
            norm(0, 0)
            rounds(pool, body)

    return nc



def block_matrices(w, name):
    rows, cols = CONVS[name][1:]
    n = FIRST[name]
    out = np.zeros((BLK, CH, len([k for k in SLOTS if k[0] == name]), BLK, CH), w.dtype)
    for (conv, m, kind, ky), slot in SLOTS.items():
        if conv != name:
            continue
        for g in range(BLK):
            row, src = rows[ky], m
            if kind == OWN:
                at = g
            elif kind == EDGE and name in PACKED:
                row, both = PACKED[name][ky]
                at = BLK if g < BLK // 2 else -1
                if g in (1, 2):
                    row += 1
                    if not both:
                        continue
            elif kind == EDGE:
                at = g + BLK if g < BLK // 2 else g - BLK
            else:
                at = -1 if kind == LEFT else BLK
                src = {"wcb": {SIDE_LL: 0, 0: 1, 1: 2, 2: 3}}.get(name, {0: 0, 1: 1, 2: 2}).get(g)
                if src is None:
                    continue
            for to in range(BLK):
                if at - to in cols:
                    tap = w[rows.index(row), cols.index(at - to)]
                    if name == "wca":
                        out[g, :, slot - n, to, :] = tap[:, src * CH:(src + 1) * CH]
                    else:
                        out[g, :, slot - n, to, :] = tap[src * CH:(src + 1) * CH, :]
    return out.reshape(P, -1, P)


def kernel(**inputs):
    import concourse.bacc as bacc
    from concourse.bass_utils import run_bass_kernel_spmd

    nc = bacc.Bacc("TRN2", target_bir_lowering=False, num_devices=1)
    a = {k.replace("L0_conv_", ""): np.ascontiguousarray(v) for k, v in inputs.items()}
    weights = np.concatenate([block_matrices(a[n], n) for n in CONVS], axis=1)
    bca = a["bca"].reshape(3, CH)
    a.update(bca0=bca[0], bca1=bca[1], bca2=bca[2])
    params = np.stack([np.tile(a[n], BLK) for n in COL], axis=1)
    code = a["L1_conv_codebook"]
    f32 = np.float32
    part = np.arange(P) % 32
    arrays = {
        "x": a["x"],
        "weights": weights,
        "params": np.ascontiguousarray(params),
        "codes4": np.ascontiguousarray(np.tile(code.T, (BLK, 1))),
        "codebook": code,
        "ident": np.eye(P, dtype=f32),
        "group_mean": np.tile(np.eye(CH, dtype=f32), (BLK, BLK)) / f32(BLK),
        "part_mask": np.stack([-(part > 0).astype(f32), -(part > 1).astype(f32)] * 2, axis=1),
    }
    names = ["x", "weights", "params", "codes4", "codebook", "ident", "group_mean", "part_mask"]
    args = [nc.dram_tensor(f"in_{n}", arrays[n].shape, F32, kind="ExternalInput").ap() for n in names]
    out = nc.dram_tensor("out", (IMAGES, HEIGHT, WIDTH, CH), F32, kind="ExternalOutput").ap()
    conv_vq_kernel(nc, *args, out)
    r = run_bass_kernel_spmd(nc, [{f"in_{n}": arrays[n] for n in names}], core_ids=[0])
    return r.results[0]["out"]
```
